# Optimizing a Trainium2 kernel written in Bass

```python
import numpy as np
import jax
import jax.numpy as jnp

def _softmax(x, axis=-1):
    return jax.nn.softmax(x, axis=axis)

def _gelu(x):
    return jax.nn.gelu(x, approximate=True)

def _silu(x):
    return jax.nn.silu(x)

def _sigmoid(x):
    return jax.nn.sigmoid(x)

def _layernorm(x, axis=-1, eps=1e-05):
    m = jnp.mean(x, axis=axis, keepdims=True)
    v = jnp.var(x, axis=axis, keepdims=True)
    return (x - m) / jnp.sqrt(v + eps)

def _scatter_add(tgt, idx, src, axis=0):
    return tgt.at[idx].add(src)

def _segment_sum(src, seg, n):
    return jax.ops.segment_sum(src, seg, n)
kernel_name = 'mk_decoder_postln_d2_seqx_r4_a55b09'

def setup_inputs(seed: int=0):
    np.random.seed(seed)
    _w = jnp.asarray

    def _rec_inputs():
        import jax
        import jax.numpy as jnp
        _rk = jax.random.key(seed)
        x = -0.0002928 + 1 * jax.random.normal(jax.random.fold_in(_rk, 1), (4, 1024, 256), jnp.float32)
        _lenS = 1024 - jax.random.randint(jax.random.fold_in(_rk, 7), (4,), 0, max(1, 1024 // 4) + 1, jnp.int32)
        _lenS2 = 77 - jax.random.randint(jax.random.fold_in(_rk, 8), (4,), 0, max(1, 77 // 4) + 1, jnp.int32)
        _ctx_1024P = jax.random.normal(jax.random.fold_in(_rk, 11), (4, 16, 256), jnp.float32)
        _ctx_1024c = jax.random.dirichlet(jax.random.fold_in(_rk, 511), 0.3 * jnp.ones((16,), jnp.float32), (4, 77))
        _ctx_1024t = jnp.einsum('bsk,bkd->bsd', _ctx_1024c, _ctx_1024P)
        _ctx_1024t = _ctx_1024t * jax.lax.rsqrt(jnp.mean(jnp.square(_ctx_1024t)) + 1e-12) * 0.953939
        ctx_1024 = -1.39393e-06 + 0.999914 * (_ctx_1024t + 0.3 * jax.random.normal(jax.random.fold_in(_rk, 611), (4, 77, 256), jnp.float32))
        return (x, ctx_1024)
    x, ctx_1024 = _rec_inputs()

    def _L0_attn_setup():
        import jax, jax.numpy as jnp
        import numpy as np
        NUM_HEADS = 8
        CHUNK = 64

        def _retention(q, k, v):
            B, Hn, L, DK = q.shape
            DV = v.shape[-1]
            C = CHUNK
            N = L // C
            dt = q.dtype
            gamma = (1.0 - jnp.exp2(-5.0 - jnp.arange(Hn, dtype=jnp.float32))).astype(dt)
            q = q * DK ** (-0.5)
            idx = jnp.arange(C)
            diff = idx[:, None] - idx[None, :]
            D = jnp.where(diff >= 0, gamma[:, None, None] ** diff, 0.0).astype(dt)
            decay_q = (gamma[:, None] ** (idx[None, :] + 1)).astype(dt)
            decay_k = (gamma[:, None] ** (C - 1 - idx[None, :])).astype(dt)
            decay_s = (gamma ** C).astype(dt)

            def to_chunks(x):
                return jnp.moveaxis(x.reshape(B, Hn, N, C, -1), 2, 0)
            qs, ks, vs = map(to_chunks, (q, k, v))

            def step(S, x):
                qc, kc, vc = x
                attn = jnp.einsum('bhid,bhjd->bhij', qc, kc) * D
                o_intra = jnp.einsum('bhij,bhje->bhie', attn, vc)
                o_inter = jnp.einsum('bhid,bhde->bhie', qc * decay_q[None, :, :, None], S)
                S_new = decay_s[None, :, None, None] * S + jnp.einsum('bhjd,bhje->bhde', kc * decay_k[None, :, :, None], vc)
                return (S_new, o_intra + o_inter)
            S0 = jnp.zeros((B, Hn, DK, DV), dt)
            _, o = jax.lax.scan(step, S0, (qs, ks, vs))
            return jnp.moveaxis(o, 0, 2).reshape(B, Hn, L, DV)

        def _xavier(key, fan_in, fan_out, gain=2 ** (-2.5)):
            limit = gain * np.sqrt(6.0 / (fan_in + fan_out))
            return jax.random.uniform(key, (fan_in, fan_out), jnp.float32, -limit, limit)
        key = jax.random.key(seed)
        k0, k1, k2, k3, k4 = jax.random.split(key, 5)
        B, L, D = (2, 1024, 256)
        return {'hidden_states': jax.random.normal(k0, (B, L, D), jnp.float32), 'rel_pos': jnp.zeros((1,), jnp.float32), 'Wq': _xavier(k1, D, D), 'Wk': _xavier(k2, D, D), 'Wv': _xavier(k3, D, D), 'Wo': _xavier(k4, D, D)}
    _L0_attn_all = _L0_attn_setup()
    _L0_attn_in = {k: v for k, v in _L0_attn_all.items() if k in ('rel_pos', 'Wq', 'Wk', 'Wv', 'Wo')}
    del _L0_attn_all

    def _L0_xattn_setup():
        import jax, jax.numpy as jnp
        import numpy as np
        D_MODEL = 256
        NUM_HEADS = 16
        HEAD_DIM = D_MODEL // NUM_HEADS
        key = jax.random.key(seed)
        kq, kk, kv, kw, kb = jax.random.split(key, 5)
        N, S = (2, 512)
        query = jax.random.normal(kq, (N, S, D_MODEL), dtype=jnp.float32)
        key_t = jax.random.normal(kk, (N, S, D_MODEL), dtype=jnp.float32)
        value = jax.random.normal(kv, (N, S, D_MODEL), dtype=jnp.float32)
        lim = 1.0 / np.sqrt(D_MODEL)
        W_out = jax.random.uniform(kw, (D_MODEL, D_MODEL), minval=-lim, maxval=lim, dtype=jnp.float32)
        b_out = jax.random.uniform(kb, (D_MODEL,), minval=-lim, maxval=lim, dtype=jnp.float32)
        return {'query': query, 'key': key_t, 'value': value, 'W_out': W_out, 'b_out': b_out}
    _L0_xattn_all = _L0_xattn_setup()
    _L0_xattn_in = {k: v for k, v in _L0_xattn_all.items() if k in ('W_out', 'b_out')}
    del _L0_xattn_all

    def _L0_ffn_setup():
        import jax, jax.numpy as jnp
        import numpy as np
        B, S, D = (4, 128, 256)
        E, K, H = (64, 8, 64)
        ES, HS = (2, 512)
        key = jax.random.key(seed)
        ks = jax.random.split(key, 8)
        scale = 0.02
        rn = lambda k, shape, s: jax.random.normal(k, shape, jnp.float32) * s
        return {'x': rn(ks[0], (B, S, D), 1.0), 'router_w': rn(ks[1], (D, E), scale), 'router_b': jnp.zeros((E,), jnp.float32), 'w1': rn(ks[2], (E, D, H), scale), 'b1': jnp.zeros((E, H), jnp.float32), 'w2': rn(ks[3], (E, H, D), scale), 'b2': jnp.zeros((E, D), jnp.float32), 'sw1': rn(ks[4], (ES, D, HS), scale), 'sb1': jnp.zeros((ES, HS), jnp.float32), 'sw2': rn(ks[5], (ES, HS, D), scale), 'sb2': jnp.zeros((ES, D), jnp.float32)}
    _L0_ffn_all = _L0_ffn_setup()
    _L0_ffn_in = {k: v for k, v in _L0_ffn_all.items() if k in ('router_w', 'router_b', 'w1', 'b1', 'w2', 'b2', 'sw1', 'sb1', 'sw2', 'sb2')}
    del _L0_ffn_all

    def _L1_attn_setup():
        import jax, jax.numpy as jnp
        import numpy as np
        HIDDEN = 256
        D_MEM = 64
        BATCH = 4
        SEQ = 256
        EPS = 1e-06

        def elu_plus_one(x):
            return jnp.where(x > 0, x + 1.0, jnp.exp(x))

        def _retrieve(sigma_x, memory, memory_norm):
            a_unnorm = jnp.matmul(sigma_x, memory)
            norm = jnp.clip(jnp.matmul(sigma_x, memory_norm), EPS, None)[..., None]
            out = a_unnorm / norm
            return jnp.where(memory_norm.sum() < EPS, jnp.zeros_like(out), out)

        def _reference_tuple_inner(hidden_states, w_q, w_k, w_v, w_o, gate, memory, memory_norm):
            b, s, _ = hidden_states.shape
            q = jnp.einsum('bsh,dh->bsd', hidden_states, w_q)
            k = jnp.einsum('bsh,dh->bsd', hidden_states, w_k)
            v = jnp.einsum('bsh,dh->bsd', hidden_states, w_v)
            sigma_q = elu_plus_one(q)
            sigma_k = elu_plus_one(k)
            memory_output = _retrieve(sigma_q, memory, memory_norm)
            kv = jnp.einsum('bsd,bse->bsde', sigma_k, v)
            kv_cumsum = jnp.cumsum(kv, axis=1)
            k_cumsum = jnp.cumsum(sigma_k, axis=1)
            numerator = jnp.einsum('bsd,bsde->bse', sigma_q, kv_cumsum)
            denominator = jnp.clip(jnp.einsum('bsd,bsd->bs', sigma_q, k_cumsum), EPS, None)[..., None]
            local_output = numerator / denominator
            g = jax.nn.sigmoid(gate[0])
            combined = g * memory_output + (1.0 - g) * local_output
            output = jnp.einsum('bsd,hd->bsh', combined, w_o)
            retrieved_unnorm = jnp.matmul(sigma_k, memory)
            norm = jnp.clip(jnp.matmul(sigma_k, memory_norm), EPS, None)[..., None]
            delta_v = v - retrieved_unnorm / norm
            memory_update = jnp.einsum('bsd,bse->de', sigma_k, delta_v) / (b * s)
            new_memory = jax.lax.stop_gradient(memory + memory_update)
            z_update = sigma_k.sum(axis=(0, 1)) / b
            new_memory_norm = jax.lax.stop_gradient(memory_norm + z_update)
            return (output, new_memory, new_memory_norm)
        key = jax.random.key(seed)
        ks = jax.random.split(key, 8)
        hidden_states = jax.random.normal(ks[0], (BATCH, SEQ, HIDDEN), dtype=jnp.float32)
        s = 1.0 / np.sqrt(HIDDEN)
        w_q = jax.random.normal(ks[1], (D_MEM, HIDDEN), dtype=jnp.float32) * s
        w_k = jax.random.normal(ks[2], (D_MEM, HIDDEN), dtype=jnp.float32) * s
        w_v = jax.random.normal(ks[3], (D_MEM, HIDDEN), dtype=jnp.float32) * s
        w_o = jax.random.normal(ks[4], (HIDDEN, D_MEM), dtype=jnp.float32) * (1.0 / np.sqrt(D_MEM))
        gate = jnp.zeros((1,), dtype=jnp.float32)
        memory = jax.random.normal(ks[5], (D_MEM, D_MEM), dtype=jnp.float32) * 0.1
        memory_norm = jax.random.uniform(ks[6], (D_MEM,), dtype=jnp.float32) * 10.0 + 1.0
        return {'hidden_states': hidden_states, 'w_q': w_q, 'w_k': w_k, 'w_v': w_v, 'w_o': w_o, 'gate': gate, 'memory': memory, 'memory_norm': memory_norm}
    _L1_attn_all = _L1_attn_setup()
    _L1_attn_in = {k: v for k, v in _L1_attn_all.items() if k in ('w_q', 'w_k', 'w_v', 'w_o', 'gate', 'memory', 'memory_norm')}
    del _L1_attn_all

    def _L1_xattn_setup():
        import jax, jax.numpy as jnp
        import numpy as np
        EMBED = 256
        HEADS = 16
        HEAD_DIM = EMBED // HEADS
        key = jax.random.key(seed)
        ks = jax.random.split(key, 7)
        B, Sd, Se = (4, 512, 512)
        dec = jax.random.normal(ks[0], (B, Sd, EMBED), dtype=jnp.float32)
        enc = jax.random.normal(ks[1], (B, Se, EMBED), dtype=jnp.float32)
        scale = 1.0 / np.sqrt(EMBED)
        W_q = jax.random.normal(ks[2], (EMBED, EMBED), dtype=jnp.float32) * scale
        W_k = jax.random.normal(ks[3], (EMBED, EMBED), dtype=jnp.float32) * scale
        W_v = jax.random.normal(ks[4], (EMBED, EMBED), dtype=jnp.float32) * scale
        W_o = jax.random.normal(ks[5], (EMBED, EMBED), dtype=jnp.float32) * scale
        b_o = jax.random.normal(ks[6], (EMBED,), dtype=jnp.float32) * 0.01
        return {'decoder_input': dec, 'encoder_output': enc, 'W_q': W_q, 'W_k': W_k, 'W_v': W_v, 'W_o': W_o, 'b_o': b_o}
    _L1_xattn_all = _L1_xattn_setup()
    _L1_xattn_in = {k: v for k, v in _L1_xattn_all.items() if k in ('W_q', 'W_k', 'W_v', 'W_o', 'b_o')}
    del _L1_xattn_all

    def _L1_ffn_setup():
        import jax, jax.numpy as jnp
        import numpy as np
        from jax import lax
        DIM = 256
        HID = 512
        E = 8
        K = 2
        B, T = (2, 128)
        key = jax.random.key(seed)
        ks = jax.random.split(key, 5)
        scale = 1.0 / np.sqrt(DIM)
        x = jax.random.normal(ks[0], (B, T, DIM), dtype=jnp.float32)
        router_w = jax.random.normal(ks[1], (E, DIM), dtype=jnp.float32) * scale
        w_gate = jax.random.normal(ks[2], (E, HID, DIM), dtype=jnp.float32) * scale
        w_up = jax.random.normal(ks[3], (E, HID, DIM), dtype=jnp.float32) * scale
        w_down = jax.random.normal(ks[4], (E, DIM, HID), dtype=jnp.float32) * (1.0 / np.sqrt(HID))
        return {'x': x, 'router_w': router_w, 'w_gate': w_gate, 'w_up': w_up, 'w_down': w_down}
    _L1_ffn_all = _L1_ffn_setup()
    _L1_ffn_in = {k: v for k, v in _L1_ffn_all.items() if k in ('router_w', 'w_gate', 'w_up', 'w_down')}
    del _L1_ffn_all
    return {'x': x, 'ctx_1024': ctx_1024, 'L0_attn_rel_pos': _L0_attn_in['rel_pos'], 'L0_attn_Wq': _L0_attn_in['Wq'], 'L0_attn_Wk': _L0_attn_in['Wk'], 'L0_attn_Wv': _L0_attn_in['Wv'], 'L0_attn_Wo': _L0_attn_in['Wo'], 'L0_xattn_W_out': _L0_xattn_in['W_out'], 'L0_xattn_b_out': _L0_xattn_in['b_out'], 'L0_ffn_router_w': _L0_ffn_in['router_w'], 'L0_ffn_router_b': _L0_ffn_in['router_b'], 'L0_ffn_w1': _L0_ffn_in['w1'], 'L0_ffn_b1': _L0_ffn_in['b1'], 'L0_ffn_w2': _L0_ffn_in['w2'], 'L0_ffn_b2': _L0_ffn_in['b2'], 'L0_ffn_sw1': _L0_ffn_in['sw1'], 'L0_ffn_sb1': _L0_ffn_in['sb1'], 'L0_ffn_sw2': _L0_ffn_in['sw2'], 'L0_ffn_sb2': _L0_ffn_in['sb2'], 'L1_attn_w_q': _L1_attn_in['w_q'], 'L1_attn_w_k': _L1_attn_in['w_k'], 'L1_attn_w_v': _L1_attn_in['w_v'], 'L1_attn_w_o': _L1_attn_in['w_o'], 'L1_attn_gate': _L1_attn_in['gate'], 'L1_attn_memory': _L1_attn_in['memory'], 'L1_attn_memory_norm': _L1_attn_in['memory_norm'], 'L1_xattn_W_q': _L1_xattn_in['W_q'], 'L1_xattn_W_k': _L1_xattn_in['W_k'], 'L1_xattn_W_v': _L1_xattn_in['W_v'], 'L1_xattn_W_o': _L1_xattn_in['W_o'], 'L1_xattn_b_o': _L1_xattn_in['b_o'], 'L1_ffn_router_w': _L1_ffn_in['router_w'], 'L1_ffn_w_gate': _L1_ffn_in['w_gate'], 'L1_ffn_w_up': _L1_ffn_in['w_up'], 'L1_ffn_w_down': _L1_ffn_in['w_down']}

def reference(x, ctx_1024, L0_attn_rel_pos, L0_attn_Wq, L0_attn_Wk, L0_attn_Wv, L0_attn_Wo, L0_xattn_W_out, L0_xattn_b_out, L0_ffn_router_w, L0_ffn_router_b, L0_ffn_w1, L0_ffn_b1, L0_ffn_w2, L0_ffn_b2, L0_ffn_sw1, L0_ffn_sb1, L0_ffn_sw2, L0_ffn_sb2, L1_attn_w_q, L1_attn_w_k, L1_attn_w_v, L1_attn_w_o, L1_attn_gate, L1_attn_memory, L1_attn_memory_norm, L1_xattn_W_q, L1_xattn_W_k, L1_xattn_W_v, L1_xattn_W_o, L1_xattn_b_o, L1_ffn_router_w, L1_ffn_w_gate, L1_ffn_w_up, L1_ffn_w_down):
    import jax
    import jax.numpy as jnp

    def _L0_attn_ref(hidden_states, rel_pos, Wq, Wk, Wv, Wo):
        import jax, jax.numpy as jnp
        import numpy as np
        NUM_HEADS = 8
        CHUNK = 64

        def _retention(q, k, v):
            B, Hn, L, DK = q.shape
            DV = v.shape[-1]
            C = CHUNK
            N = L // C
            dt = q.dtype
            gamma = (1.0 - jnp.exp2(-5.0 - jnp.arange(Hn, dtype=jnp.float32))).astype(dt)
            q = q * DK ** (-0.5)
            idx = jnp.arange(C)
            diff = idx[:, None] - idx[None, :]
            D = jnp.where(diff >= 0, gamma[:, None, None] ** diff, 0.0).astype(dt)
            decay_q = (gamma[:, None] ** (idx[None, :] + 1)).astype(dt)
            decay_k = (gamma[:, None] ** (C - 1 - idx[None, :])).astype(dt)
            decay_s = (gamma ** C).astype(dt)

            def to_chunks(x):
                return jnp.moveaxis(x.reshape(B, Hn, N, C, -1), 2, 0)
            qs, ks, vs = map(to_chunks, (q, k, v))

            def step(S, x):
                qc, kc, vc = x
                attn = jnp.einsum('bhid,bhjd->bhij', qc, kc) * D
                o_intra = jnp.einsum('bhij,bhje->bhie', attn, vc)
                o_inter = jnp.einsum('bhid,bhde->bhie', qc * decay_q[None, :, :, None], S)
                S_new = decay_s[None, :, None, None] * S + jnp.einsum('bhjd,bhje->bhde', kc * decay_k[None, :, :, None], vc)
                return (S_new, o_intra + o_inter)
            S0 = jnp.zeros((B, Hn, DK, DV), dt)
            _, o = jax.lax.scan(step, S0, (qs, ks, vs))
            return jnp.moveaxis(o, 0, 2).reshape(B, Hn, L, DV)

        def _xavier(key, fan_in, fan_out, gain=2 ** (-2.5)):
            limit = gain * np.sqrt(6.0 / (fan_in + fan_out))
            return jax.random.uniform(key, (fan_in, fan_out), jnp.float32, -limit, limit)
        B, L, Dm = hidden_states.shape
        Hd = Dm // NUM_HEADS
        q = (hidden_states @ Wq).reshape(B, L, NUM_HEADS, Hd).transpose(0, 2, 1, 3)
        k = (hidden_states @ Wk).reshape(B, L, NUM_HEADS, Hd).transpose(0, 2, 1, 3)
        v = (hidden_states @ Wv).reshape(B, L, NUM_HEADS, Hd).transpose(0, 2, 1, 3)
        o = _retention(q, k, v)
        o = o.transpose(0, 2, 1, 3).reshape(B, L, Dm)
        return o @ Wo

    def _L0_xattn_ref(query, key, value, W_out, b_out):
        import jax, jax.numpy as jnp
        import numpy as np
        D_MODEL = 256
        NUM_HEADS = 16
        HEAD_DIM = D_MODEL // NUM_HEADS
        N, Lq, _ = query.shape
        Lk = key.shape[1]
        q = query.reshape(N, Lq, NUM_HEADS, HEAD_DIM)
        k = key.reshape(N, Lk, NUM_HEADS, HEAD_DIM)
        v = value.reshape(N, Lk, NUM_HEADS, HEAD_DIM)
        scores = jnp.einsum('nqhd,nkhd->nhqk', q, k)
        attn = jax.nn.softmax(scores, axis=3)
        out = jnp.einsum('nhqk,nkhd->nqhd', attn, v).reshape(N, Lq, D_MODEL)
        return out @ W_out.T + b_out

    def _L0_ffn_ref(x, router_w, router_b, w1, b1, w2, b2, sw1, sb1, sw2, sb2):
        import jax, jax.numpy as jnp
        import numpy as np
        B, S, D = (4, 128, 256)
        E, K, H = (64, 8, 64)
        ES, HS = (2, 512)
        b_, s_, d_ = x.shape
        xf = x.reshape(-1, d_)
        probs = jax.nn.softmax(xf @ router_w + router_b, axis=-1)
        tw, ti = jax.lax.top_k(probs, K)
        tw = tw / jnp.sum(tw, axis=-1, keepdims=True)

        def body(acc, p):
            W1, B1, W2, B2, e = p
            h = jax.nn.silu(xf @ W1 + B1) @ W2 + B2
            cw = jnp.sum(jnp.where(ti == e, tw, 0.0), axis=-1)
            return (acc + cw[:, None] * h, None)
        routed, _ = jax.lax.scan(body, jnp.zeros_like(xf), (w1, b1, w2, b2, jnp.arange(w1.shape[0])))

        def shared_mlp(W1, B1, W2, B2):
            return jax.nn.silu(xf @ W1 + B1) @ W2 + B2
        shared = jnp.sum(jax.vmap(shared_mlp)(sw1, sb1, sw2, sb2), axis=0)
        return (routed + shared).reshape(b_, s_, d_)

    def _L1_attn_ref(hidden_states, w_q, w_k, w_v, w_o, gate, memory, memory_norm):
        import jax, jax.numpy as jnp
        import numpy as np
        HIDDEN = 256
        D_MEM = 64
        BATCH = 4
        SEQ = 256
        EPS = 1e-06

        def elu_plus_one(x):
            return jnp.where(x > 0, x + 1.0, jnp.exp(x))

        def _retrieve(sigma_x, memory, memory_norm):
            a_unnorm = jnp.matmul(sigma_x, memory)
            norm = jnp.clip(jnp.matmul(sigma_x, memory_norm), EPS, None)[..., None]
            out = a_unnorm / norm
            return jnp.where(memory_norm.sum() < EPS, jnp.zeros_like(out), out)

        def _reference_tuple_inner(hidden_states, w_q, w_k, w_v, w_o, gate, memory, memory_norm):
            b, s, _ = hidden_states.shape
            q = jnp.einsum('bsh,dh->bsd', hidden_states, w_q)
            k = jnp.einsum('bsh,dh->bsd', hidden_states, w_k)
            v = jnp.einsum('bsh,dh->bsd', hidden_states, w_v)
            sigma_q = elu_plus_one(q)
            sigma_k = elu_plus_one(k)
            memory_output = _retrieve(sigma_q, memory, memory_norm)
            kv = jnp.einsum('bsd,bse->bsde', sigma_k, v)
            kv_cumsum = jnp.cumsum(kv, axis=1)
            k_cumsum = jnp.cumsum(sigma_k, axis=1)
            numerator = jnp.einsum('bsd,bsde->bse', sigma_q, kv_cumsum)
            denominator = jnp.clip(jnp.einsum('bsd,bsd->bs', sigma_q, k_cumsum), EPS, None)[..., None]
            local_output = numerator / denominator
            g = jax.nn.sigmoid(gate[0])
            combined = g * memory_output + (1.0 - g) * local_output
            output = jnp.einsum('bsd,hd->bsh', combined, w_o)
            retrieved_unnorm = jnp.matmul(sigma_k, memory)
            norm = jnp.clip(jnp.matmul(sigma_k, memory_norm), EPS, None)[..., None]
            delta_v = v - retrieved_unnorm / norm
            memory_update = jnp.einsum('bsd,bse->de', sigma_k, delta_v) / (b * s)
            new_memory = jax.lax.stop_gradient(memory + memory_update)
            z_update = sigma_k.sum(axis=(0, 1)) / b
            new_memory_norm = jax.lax.stop_gradient(memory_norm + z_update)
            return (output, new_memory, new_memory_norm)
        return _reference_tuple_inner(hidden_states, w_q, w_k, w_v, w_o, gate, memory, memory_norm)[0]

    def _L1_xattn_ref(decoder_input, encoder_output, W_q, W_k, W_v, W_o, b_o):
        import jax, jax.numpy as jnp
        import numpy as np
        EMBED = 256
        HEADS = 16
        HEAD_DIM = EMBED // HEADS
        B, Sd, E = decoder_input.shape
        Se = encoder_output.shape[1]
        Q = (decoder_input @ W_q).reshape(B, Sd, HEADS, HEAD_DIM)
        K = (encoder_output @ W_k).reshape(B, Se, HEADS, HEAD_DIM)
        V = (encoder_output @ W_v).reshape(B, Se, HEADS, HEAD_DIM)
        scores = jnp.einsum('bqhd,bkhd->bhqk', Q, K) / jnp.sqrt(jnp.float32(HEAD_DIM))
        attn = jax.nn.softmax(scores, axis=-1)
        out = jnp.einsum('bhqk,bkhd->bqhd', attn, V).reshape(B, Sd, E)
        return out @ W_o + b_o

    def _L1_ffn_ref(x, router_w, w_gate, w_up, w_down):
        import jax, jax.numpy as jnp
        import numpy as np
        from jax import lax
        DIM = 256
        HID = 512
        E = 8
        K = 2
        B, T = (2, 128)
        Bb, Tt, D = x.shape
        N = Bb * Tt
        xf = x.reshape(N, D)
        logits = xf @ router_w.T
        routing = jax.nn.softmax(logits, axis=-1)
        top_w, top_i = lax.top_k(routing, K)
        top_w = top_w / jnp.sum(top_w, axis=-1, keepdims=True)
        combine = jnp.zeros((N, E), dtype=x.dtype)
        combine = combine.at[jnp.arange(N)[:, None], top_i].add(top_w)
        g = jnp.einsum('nd,ehd->neh', xf, w_gate)
        u = jnp.einsum('nd,ehd->neh', xf, w_up)
        h = jax.nn.silu(g) * u
        y = jnp.einsum('neh,edh->ned', h, w_down)
        out = jnp.einsum('ned,ne->nd', y, combine)
        return out.reshape(Bb, Tt, D)
    x = _layernorm(x + _L0_attn_ref(x, L0_attn_rel_pos, L0_attn_Wq, L0_attn_Wk, L0_attn_Wv, L0_attn_Wo), axis=-1)
    x = _layernorm(x + _L0_xattn_ref(x, ctx_1024, ctx_1024, L0_xattn_W_out, L0_xattn_b_out), axis=-1)
    x = _layernorm(x + _L0_ffn_ref(x, L0_ffn_router_w, L0_ffn_router_b, L0_ffn_w1, L0_ffn_b1, L0_ffn_w2, L0_ffn_b2, L0_ffn_sw1, L0_ffn_sb1, L0_ffn_sw2, L0_ffn_sb2), axis=-1)
    x = _layernorm(x + _L1_attn_ref(x, L1_attn_w_q, L1_attn_w_k, L1_attn_w_v, L1_attn_w_o, L1_attn_gate, L1_attn_memory, L1_attn_memory_norm), axis=-1)
    x = _layernorm(x + _L1_xattn_ref(x, ctx_1024, L1_xattn_W_q, L1_xattn_W_k, L1_xattn_W_v, L1_xattn_W_o, L1_xattn_b_o), axis=-1)
    x = _layernorm(x + _L1_ffn_ref(x, L1_ffn_router_w, L1_ffn_w_gate, L1_ffn_w_up, L1_ffn_w_down), axis=-1)
    return x

_drawn_inputs = setup_inputs


def setup_inputs(seed=0):
    import zlib

    import numpy as np

    out = dict(_drawn_inputs(seed))
    spreads = {'L0_ffn_router_b': (0.0, 0.1),
     'L0_ffn_b1': (0.0, 0.462),
     'L0_ffn_b2': (0.0, 0.1),
     'L0_ffn_sb1': (0.0, 0.1),
     'L0_ffn_sb2': (0.0, 0.1)}
    factors = {'L1_attn_w_q': 4.23,
     'L1_attn_w_k': 3.548,
     'L1_attn_memory': 8.0,
     'L1_attn_memory_norm': 8.0}
    for name, (base, spread) in spreads.items():
        noise = np.random.default_rng([zlib.crc32(name.encode()), seed]).standard_normal(out[name].shape)
        drawn = base * np.exp(spread * noise) if base else spread * noise
        out[name] = jnp.asarray(drawn.astype(out[name].dtype))
    for name, factor in factors.items():
        out[name] = (out[name] * factor).astype(out[name].dtype)
    return out
```

```python
from contextlib import ExitStack

import numpy as np
import concourse.bass as bass
from concourse import mybir

F32 = mybir.dt.float32
ALU = mybir.AluOpType
ACT = mybir.ActivationFunctionType
AX = mybir.AxisListType

P = 128
NB, SEQ, DM = 4, 1024, 256
NT = NB * SEQ
KC = DM // P
CTX = 77
XH, XD = 16, 16
VW = XD + 1
QH = 4 * CTX
RH, RD = 8, 32
MEM = 64
STEPS = SEQ // P
LN_EPS = 1e-5
CLIP = 1e-6


class BankPlan:

    def __init__(self, jobs, banks, uses_before=None):
        self.banks = banks
        self.place, self.uses = {}, {k: 0 for k in banks}
        for n, job in enumerate(jobs):
            k = banks[n % len(banks)]
            self.place[job] = (k, self.uses[k])
            self.uses[k] += 1

    def bank(self, job):
        return self.place[job][0]

    def before(self, job, i):
        k, n = self.place[job]
        return i * self.uses[k] + n

    def after(self, job, i):
        return self.before(job, i) + 1


class Chain:

    def __init__(self, eng, sem, per_pass):
        self.eng, self.sem, self.n, self.count, self.base = eng, sem, per_pass, 0, 0

    def start(self, i):
        assert self.count in (0, self.n), (self.count, self.n)
        self.base, self.count = i * self.n, 0

    def __call__(self, ins, carrier=None):
        self.count += 1
        ins.then_inc(self.sem, 1)
        self.eng.wait_ge(self.sem, self.base + self.count)
        if carrier is not None:
            carry(self.eng, carrier)


def carry(dve, spot):
    dve.memset(spot, 0.0)


def wavefront(groups):
    order = []
    for group in groups:
        for step in range(NB + len(group) - 1):
            for k, stage in enumerate(group):
                if 0 <= step - k < NB:
                    order.append((stage, step - k))
    return order


VCHAIN = {0: 36, 1: 64}
VPREP = {0: 12, 1: 25}


def attention_phase(nc, sems, layer, d, src, src_t, dst, dst_t, dst_cw, experts, top, prefetch, spare):
    first = layer == 0
    if first:
        groups = [["qkv"], ["ret", "mix"], ["wo"], ["ln1"], ["x1t"], ["sc", "pt", "pv"], ["at"], ["wout"],
                  ["ln2"], ["x2t"], ["rt"], ["top"], ["cwt"], ["b2"]]
        banks_of = {"qkv": 2, "ret": 4, "mix": 2, "wo": 1, "x1t": 1, "sc": 4, "pt": 4, "pv": 1, "at": 1,
                    "wout": 1, "x2t": 1, "rt": 1, "cwt": 1, "b2": 1}
    else:
        groups = [["x0t"], ["lin"], ["tri"], ["num"], ["ct"], ["wo"], ["ln1"], ["x1t"], ["q"],
                  ["sc", "pt", "pv"], ["at"], ["wout"], ["ln2"], ["x2t"], ["rt"], ["top"]]
        banks_of = {"x0t": 1, "lin": 2, "tri": 1, "num": 2, "ct": 1, "wo": 1, "x1t": 1, "q": 1, "sc": 4,
                    "pt": 4, "pv": 1, "at": 1, "wout": 1, "x2t": 1, "rt": 1}
    order = wavefront(groups)
    plan = BankPlan([(s, b, n) for s, b in order for n in range(banks_of.get(s, 0))], list(range(8)))
    score_scale = 1.0 if first else float(XD) ** -0.5
    E = experts

    with ExitStack() as ctx:
        def sb(name, shape):
            return ctx.enter_context(nc.sbuf_tensor(f"{name}_{layer}", shape, F32))

        def sem(name):
            return sems.enter_context(nc.semaphore(f"{name}_{layer}"))

        psum = [ctx.enter_context(nc.psum_tensor(f"bank{k}_{layer}", [P, 512], F32)) for k in range(8)]

        ident = sb("ident", [P, P])
        head_mask = sb("head_mask", [P, P // XD])
        keys = spare[:, 0:NB * KC * 8 * CTX].rearrange("p (b g n) -> p b g n", b=NB, g=KC)
        vals = sb("vals", [CTX, NB, XH, VW])
        wout = sb("wout", [P, KC, DM])
        bout = sb("bout", [P, DM])
        router = sb("router", [P, KC, E])
        half = sb("half", [P, 1])
        eps = sb("eps", [P, 1])
        spot = sb("spot", [P, 1])
        if first:
            decay = sb("decay", [P, 4, 2, P])
            decay_q = sb("decay_q", [P, 2, P])
            decay_k = sb("decay_k", [P, DM])
            decay_s = sb("decay_s", [P, 2])
            block_mask = sb("block_mask", [P, P])
            wqkv = sb("wqkv", [P, KC, 3 * DM])
            wqk, wkv = wqkv[:, :, 0:2 * DM], wqkv[:, :, DM:3 * DM]
            wo = sb("wo", [P, KC, DM])
            ones = sb("ones", [1, P])
            router_b = sb("router_b", [1, E])
            b2 = sb("b2", [E, DM])
            sb2 = sb("sb2", [P, 2, DM])
            ctx_t = sb("ctx_t", [P, NB, KC, CTX])
            state = sb("state", [P, NB, 2, P])
        else:
            causal = sb("causal", [P, P])
            wqk = sb("wqk", [P, KC, 2 * MEM])
            wkv = sb("wkv", [P, KC, 2 * MEM])
            wo = sb("wo", [MEM, DM])
            wq = sb("wq", [P, KC, DM])
            wk = sb("wk", [P, KC, DM])
            wv = sb("wv", [P, KC, DM])
            ctx_t = sb("ctx_t", [P, NB, KC, CTX])
            key_t = sb("key_t", [P, NB, KC, CTX])
            memory = sb("memory", [MEM, MEM + 1])
            mem_norm = sb("mem_norm", [P, MEM])
            gate = sb("gate", [P, 1])
            mixw = sb("mixw", [P, 2])
            small = sb("small", [P, 4])
            iota = sb("iota", [P, E])
            state = sb("state", [MEM, NB, MEM + 1])

        x = sb("x", [P, NB, DM])
        xt = sb("xt", [P, NB, KC, P])
        x1 = sb("x1", [P, NB, DM])
        x1b = sb("x1b", [P, NB, DM])
        x1t = sb("x1t", [P, NB, KC, P])
        if first:
            qk = sb("qk", [P, NB, 4, P])
            qd = sb("qd", [P, NB, 2, P])
            kd = sb("kd", [P, NB, DM])
            v = sb("v", [P, NB, DM])
            ot = qd
            upd = sb("upd", [P, 2, P])
            cwt = sb("cwt", [E, NB, P])
            xr = sb("xr", [P, NB, DM])
        else:
            neg_rows = sb("neg_t", [P, NB, 2 * P])
            neg_t = neg_rows[0:MEM]
            neg = sb("neg", [P, NB, MEM])
            sig = sb("sig", [MEM, NB, 2, P])
            sigk = sb("sigk", [P, NB, MEM])
            v = sb("v", [P, NB, MEM + 1])
            tri = sb("tri", [P, NB, P])
            den = sb("den", [P, NB, 6])
            comb = sb("comb", [P, NB, MEM])
            combt = sb("combt", [MEM, NB, P])
            qt = sb("qt", [P, NB, KC, P])
            top_i = sb("top_i", [P, NB, 8])
            top_u = ctx.enter_context(nc.sbuf_tensor(f"top_u_{layer}", [P, NB, 8], mybir.dt.uint32))
            hot = sb("hot", [P, NB, 2, E])
        z = sb("z", [P, NB, DM])
        stats = sb("stats", [P, NB, 6])
        mv = sb("mv", [P, NB, 4])
        peak = sb("peak", [P, 2, XH])
        s = sb("s", [P, 2, XH * CTX])
        pt = sb("pt", [CTX, 2, XH, P])
        if first:
            prob = s[:, :, 0:4 * 2 * P].rearrange("p a (r g n) -> p a r g n", r=4, g=2)
        rsum = sb("rsum", [P, NB, XH])
        att, att_t = z, x1t
        x2 = sb("x2", [P, NB, DM])
        x2t = sb("x2t", [P, NB, KC, P])
        nmax = sb("nmax", [P, NB, 1])
        ex = sb("ex", [P, NB, E])
        top8 = sb("top8", [P, NB, 8])
        rest = sb("rest", [P, NB, E])
        tsum = sb("tsum", [P, NB, 2])
        cw = sb("cw", [P, NB, E])

        full = [sem(f"full{k}") for k in range(8)]
        free = [sem(f"free{k}") for k in range(8)]
        consts = sem("consts")
        x_in = [sem(f"x_in{b}") for b in range(NB)]
        xt_in = [sem(f"xt_in{b}") for b in range(NB)] if first else None
        sent = [sem(f"sent{b}") for b in range(NB)]
        prep = sem("prep")
        prep_pe = None if first else sem("prep_pe")
        prep_pool = sem("prep_pool")
        gate_exp = None if first else sem("gate_exp")
        vchain = sem("vchain")
        gchain = sem("gchain")
        moved = sem("moved")
        qkd_done = sem("qkd_done") if first else None
        state_done = sem("state_done")
        o_moved = sem("o_moved") if first else None
        mv1_done = sem("mv1_done")
        rstd1 = sem("rstd1")
        x1_done = sem("x1_done")
        x1b_done = sem("x1b_done")
        x1t_done = sem("x1t_done")
        s_done = sem("s_done")
        exp_done = sem("exp_done")
        pta_done = sem("pta_done")
        att_done = sem("att_done")
        att_t_done = sem("att_t_done")
        mv2_done = sem("mv2_done")
        rstd2 = sem("rstd2")
        x2_done = sem("x2_done")
        x2s_done = sem("x2s_done") if first else None
        x2t_done = sem("x2t_done")
        nmax_done = sem("nmax_done")
        ex_done = sem("ex_done")
        cw_done = sem("cw_done")
        cwt_done = sem("cwt_done") if first else None
        xr_done = sem("xr_done") if first else None
        neg_done = None if first else sem("neg_done")
        nexp_done = None if first else sem("nexp_done")
        combt_done = None if first else sem("combt_done")
        q_done = None if first else sem("q_done")

        def nth(i, b):
            return i * NB + b + 1

        def col(t):
            return t.rearrange("(c p) n -> p c n", p=P)

        loads = [(ident[:], d["ident"]), (head_mask[:], d["head_mask"]), (wout[:], col(d["wout"])),
                 (bout[:], d["bout"]), (router[:], col(d["router"])),
                 (ctx_t[:], d["ctx_t"].rearrange("b (c p) n -> p b c n", p=P))]
        if first:
            loads += [(wqkv[:, :, 0:DM], col(d["wq"])), (wqkv[:, :, DM:2 * DM], col(d["wk"])),
                      (wqkv[:, :, 2 * DM:], col(d["wv"])),
                      (wo[:], col(d["wo"])), (decay[:], d["decay"]), (decay_q[:], d["decay_q"]),
                      (decay_k[:], d["decay_k"]), (decay_s[:], d["decay_s"]), (block_mask[:], d["block_mask"]),
                      (router_b[:], d["router_b"]), (b2[:], d["b2"]), (sb2[:], d["sb2"])]
            loads += [(vals[:, b, :, 0:XD], d["ctx"][b].rearrange("k (h e) -> k h e", e=XD)) for b in range(NB)]
        else:
            loads += [(wqk[:, :, 0:MEM], col(d["wq1"])), (wqk[:, :, MEM:], col(d["wk1"])),
                      (wkv[:, :, 0:MEM], col(d["wk1"])), (wkv[:, :, MEM:], col(d["wv1"])),
                      (wo[:], d["wo1"]), (causal[:], d["causal"]), (wq[:], col(d["wq"])),
                      (wk[:], col(d["wk"])), (wv[:], col(d["wv"])),
                      (memory[:, 0:MEM], d["memory"]), (memory[:, MEM:], d["mem_norm"]),
                      (mem_norm[:], d["mem_norm_rows"]), (gate[:], d["gate"]), (iota[:], d["iota"])]

        signals = {("qkv", 0): (moved, 1, 1, 0), ("x0t", 0): (moved, 1, 1, 0), ("mix", 0): (o_moved, 1, 1, 0),
                   ("ct", 0): (combt_done, 1, 1, 0), ("x1t", 0): (x1t_done, 1, 1, 0), ("q", 0): (q_done, 1, 1, 0),
                   ("pt", 0): (pta_done, 2, 1, 0), ("pt", 1): (pta_done, 2, 2, 0), ("at", 0): (att_t_done, 1, 1, 0),
                   ("x2t", 0): (x2t_done, 1, 1, 0), ("rt", 0): (ex_done, 1, 1, 0), ("cwt", 0): (cwt_done, 1, 1, 0),
                   ("num", 1): (state_done, 1, 1, NB), ("sc", 3): (s_done, 1, 1, 0), ("pv", 0): (att_done, 1, 1, 0),
                   ("b2", 0): (xr_done, 1, 1, 0)}
        by_place = {place: job for job, place in plan.place.items()}
        unsignalled = {k: [by_place[(k, n)] for n in range(plan.uses[k])
                           if (by_place[(k, n)][0], by_place[(k, n)][2]) not in signals] for k in range(8)}

        def freed(eng, job, i):
            stage, b, n = job
            if (stage, n) in signals:
                signal, per, at, ahead = signals[(stage, n)]
                eng.wait_ge(signal, (i * NB + b) * per + at + ahead)
            else:
                k = plan.bank(job)
                eng.wait_ge(free[k], i * len(unsignalled[k]) + unsignalled[k].index(job) + 1)

        def freed_before(eng, k, i):
            stage, b, n = by_place[(k, plan.uses[k] - 1)]
            if (stage, n) in signals:
                signal, per, at, ahead = signals[(stage, n)]
                eng.wait_ge(signal, i * (NB * per) + ahead)
            else:
                eng.wait_ge(free[k], i * len(unsignalled[k]))

        block = ctx.enter_context(nc.Block())

        @block.sync
        def _(sp):
            def load(b, span):
                sp.dma_start(x[:, b, :], src[b, span, :]).then_inc(x_in[b], 16)
                if first:
                    cols = src_t[b, :, span]
                    sp.dma_start(xt[:, b], cols.rearrange("(c p) n -> p c n", p=P)).then_inc(xt_in[b], 16)

            for dst_ap, src_ap in loads:
                sp.dma_start(dst_ap, src_ap).then_inc(consts, 16)
            for b in range(NB):
                load(b, slice(0, P))
            prefetch(sp)
            with sp.Fori(1, STEPS) as i:
                for b in range(NB):
                    freed(sp, ("wo", b, 0), i - 1)
                    if first:
                        job = ("qkv", b, 1)
                        sp.wait_ge(full[plan.bank(job)], plan.after(job, i - 1))
                    load(b, bass.ds(i * P, P))

        def out_dmas(eng, i, b, what):
            rows = bass.ds(b * SEQ + i * P, P)
            if what == "cols":
                eng.wait_ge(x2t_done, nth(i, b))
                eng.dma_start(dst_t[:, rows].rearrange("(c p) n -> p c n", p=P), x2t[:, b]).then_inc(sent[b], 16)
            if what == "cw":
                eng.wait_ge(cw_done, nth(i, b))
                eng.dma_start(dst_cw[rows, :], cw[:, b, :]).then_inc(sent[b], 16)
            if what == "rows":
                eng.wait_ge(xr_done if first else x2_done, nth(i, b))
                eng.dma_start(dst[rows, :], (xr if first else x2)[:, b, :]).then_inc(sent[b], 16)

        @block.gpsimd
        def _(pool):
            chain = Chain(pool, gchain, 2 * NB)
            nc.gpsimd.memset(half[:], -0.5)
            nc.gpsimd.memset(eps[:], LN_EPS).then_inc(prep_pool, 1)
            if first:
                nc.gpsimd.memset(ones[:], 1.0).then_inc(prep_pool, 1)
            pool.wait_ge(prep_pool, 2 if first else 1)
            pool.wait_ge(consts, 16 * len(loads))
            if first:
                nc.gpsimd.tensor_tensor(sb2[:, 0], sb2[:, 0], sb2[:, 1], ALU.add).then_inc(prep_pool, 1)
                pool.wait_ge(prep_pool, 3)
            with pool.Fori(0, STEPS) as i:
                chain.start(i)
                for stage, b in order:
                    if stage in ("wo", "wout"):
                        one = stage == "wo"
                        pool.wait_ge(mv1_done if one else mv2_done, nth(i, b))
                        chain(nc.gpsimd.tensor_tensor(mv[:, b, 2:3], mv[:, b, 1:2], eps[:], ALU.add))
                        nc.gpsimd.tensor_tensor(mv[:, b, 3:4], mv[:, b, 2:3], half[:], ALU.pow)\
                            .then_inc(rstd1 if one else rstd2, 1)
                    if stage == "ln1":
                        pool.wait_ge(x1_done, nth(i, b))
                        nc.gpsimd.tensor_tensor(x1b[:, b], x1[:, b], bout[:], ALU.add).then_inc(x1b_done, 1)
                    if stage == "ln2" and first:
                        pool.wait_ge(x2_done, nth(i, b))
                        nc.gpsimd.tensor_tensor(x1b[:, b], x2[:, b], sb2[:, 0], ALU.add).then_inc(x2s_done, 1)
                for b in range(NB):
                    out_dmas(pool, i, b, "cols")
                for b in range(NB):
                    out_dmas(pool, i, b, "cw")
                for b in range(NB):
                    out_dmas(pool, i, b, "rows")
            for b in range(NB):
                pool.wait_ge(sent[b], 48 * STEPS)

        @block.scalar
        def _(act):
            if not first:
                act.wait_ge(consts, 16 * len(loads))
                nc.scalar.activation(small[:, 0:1], gate[:], ACT.Exp, scale=-1.0).then_inc(gate_exp, 1)
            with act.Fori(0, STEPS) as i:
                for stage, b in order:
                    def bank(n=0, stage=stage, b=b):
                        job = (stage, b, n)
                        act.wait_ge(full[plan.bank(job)], plan.after(job, i))
                        return psum[plan.bank(job)]

                    def move(out, in_, done):
                        nc.scalar.activation(out, in_, ACT.Copy).then_inc(done, 1)

                    if stage == "qkv":
                        move(qk[:, b], bank(0)[:].rearrange("p (a n) -> p a n", a=4), moved)
                    if stage == "x0t":
                        move(xt[:, b], bank()[:, 0:DM].rearrange("p (c n) -> p c n", c=KC), moved)
                    if stage == "mix":
                        move(ot[:, b], bank(0)[:, 0:2 * P].rearrange("p (g n) -> p g n", g=2), o_moved)
                    if stage == "lin":
                        act.wait_ge(neg_done, nth(i, b))
                        nc.scalar.activation(neg_t[:, b], neg_t[:, b], ACT.Exp)
                        nc.scalar.activation(neg[:, b], neg[:, b], ACT.Exp)\
                            .then_inc(nexp_done, 1)
                    if stage == "ct":
                        move(combt[:, b], bank()[0:MEM, 0:P], combt_done)
                    if stage == "x1t":
                        move(x1t[:, b], bank()[:, 0:DM].rearrange("p (c n) -> p c n", c=KC), x1t_done)
                    if stage == "q":
                        move(qt[:, b], bank()[:, 0:DM].rearrange("p (c n) -> p c n", c=KC), q_done)
                    if stage == "sc":
                        act.wait_ge(s_done, nth(i, b))
                        nc.scalar.activation(s[:, b % 2], s[:, b % 2], ACT.Exp, scale=score_scale)\
                            .then_inc(exp_done, 1)
                    if stage == "pt":
                        for n in (0, 1):
                            move(pt[:, b % 2, 4 * n:4 * n + 4], bank(n)[0:CTX, :].rearrange("p (h n) -> p h n", h=4),
                                 pta_done)
                    if stage == "at":
                        move(att_t[:, b], bank()[:, 0:DM].rearrange("p (c n) -> p c n", c=KC), att_t_done)
                    if stage == "x2t":
                        act.wait_ge(sent[b], i * 48)
                        move(x2t[:, b], bank()[:, 0:DM].rearrange("p (c n) -> p c n", c=KC), x2t_done)
                    if stage == "rt":
                        act.wait_ge(nmax_done, nth(i, b))
                        nc.scalar.activation(ex[:, b], bank()[:, 0:E], ACT.Exp, bias=nmax[:, b])\
                            .then_inc(ex_done, 1)
                    if stage == "cwt":
                        move(cwt[:, b], bank()[0:E, 0:P], cwt_done)

        @block.vector
        def _(dve):
            chain = Chain(dve, vchain, VCHAIN[layer])
            plain = [0]

            def done(ins):
                plain[0] += 1
                ins.then_inc(prep, 1)
                dve.wait_ge(prep, plain[0])

            for b in range(NB):
                nc.vector.memset(state[:, b], 0.0).then_inc(state_done, 1)
            if not first:
                done(nc.vector.memset(v[:], 1.0))
                done(nc.vector.memset(neg_rows[:], 0.0))
                done(nc.vector.memset(vals[:], 1.0))
            dve.wait_ge(consts, 16 * len(loads))
            if first:
                for b in range(NB):
                    done(nc.vector.memset(vals[:, b, :, XD:], 1.0))
            else:
                dve.wait_ge(gate_exp, 1)
                done(nc.vector.tensor_scalar(small[:, 1:2], small[:, 0:1], 1.0, None, ALU.add))
                done(nc.vector.reciprocal(small[:, 2:3], small[:, 1:2]))
                done(nc.vector.tensor_scalar(mixw[:, 0:1], small[:, 2:3], -1.0, 1.0, ALU.mult, ALU.add))
                done(nc.vector.tensor_reduce(small[:, 3:4], mem_norm[:], AX.X, ALU.add))
                done(nc.vector.tensor_scalar(small[:, 3:4], small[:, 3:4], CLIP, None, ALU.is_ge))
                done(nc.vector.tensor_tensor(mixw[:, 1:2], small[:, 3:4], small[:, 2:3], ALU.mult))
                for b in range(NB):
                    dve.wait_ge(prep_pe, 1 + 2 * b)
                    done(nc.vector.tensor_copy(key_t[:, b], psum[2 * b][:, 0:KC * CTX]
                                               .rearrange("p (c n) -> p c n", c=KC)))
                    dve.wait_ge(prep_pe, 2 + 2 * b)
                    done(nc.vector.tensor_copy(vals[:, b, :, 0:XD], psum[2 * b + 1][0:CTX, 0:DM]
                                               .rearrange("p (h e) -> p h e", e=XD)))
            for b in range(NB):
                for g in range(KC):
                    kin = (ctx_t if first else key_t)[:, b, g].unsqueeze(1).broadcast_to([P, 8, CTX])
                    mask = head_mask[:].unsqueeze(2).broadcast_to([P, 8, CTX])
                    done(nc.vector.tensor_tensor(keys[:, b, g].rearrange("p (h k) -> p h k", h=8),
                                                 kin, mask, ALU.mult))
            assert plain[0] == VPREP[layer], plain[0]

            with dve.Fori(0, STEPS) as i:
                chain.start(i)
                for stage, b in order:
                    def bank(n=0, stage=stage, b=b):
                        job = (stage, b, n)
                        dve.wait_ge(full[plan.bank(job)], plan.after(job, i))
                        return psum[plan.bank(job)]

                    def frees(ins, n=0, stage=stage, b=b):
                        ins.then_inc(free[plan.bank((stage, b, n))], 1)

                    def norm_sums(rows, done_sem):
                        frees(nc.vector.tensor_tensor(z[:, b], bank()[:, 0:DM], rows, ALU.add))
                        freed(dve, (stage, b, 0), i)
                        chain(nc.vector.bn_stats(stats[:, b], z[:, b]), carrier=spot[:])
                        nc.vector.bn_aggr(mv[:, b, 0:2], stats[:, b]).then_inc(done_sem, 1)

                    def norm(out, rstd, done_sem):
                        dve.wait_ge(rstd, nth(i, b))
                        nc.vector.tensor_scalar(out, z[:, b], mv[:, b, 0:1], mv[:, b, 3:4],
                                                ALU.subtract, ALU.mult).then_inc(done_sem, 1)

                    if stage == "qkv":
                        kv = bank(1)
                        nc.vector.tensor_tensor(kd[:, b], kv[:, 0:DM], decay_k[:], ALU.mult)
                        frees(nc.vector.tensor_copy(v[:, b], kv[:, DM:2 * DM]), 1)
                        dve.wait_ge(moved, nth(i, b))
                        nc.vector.tensor_tensor(qd[:, b], qk[:, b, 0:2], decay_q[:], ALU.mult).then_inc(qkd_done, 1)
                    if stage == "ret":
                        for n in range(4):
                            frees(nc.vector.tensor_tensor(prob[:, b % 2, n],
                                                          bank(n)[:, 0:2 * P].rearrange("p (g n) -> p g n", g=2),
                                                          decay[:, n], ALU.mult), n)
                    if stage == "mix":
                        dve.wait_ge(state_done, nth(i, b) + NB - 1)
                        frees(nc.vector.tensor_tensor(upd[:], bank(1)[:, 0:2 * P].rearrange("p (g n) -> p g n", g=2),
                                                      block_mask[:].unsqueeze(1).broadcast_to([P, 2, P]),
                                                      ALU.mult), 1)
                        freed(dve, ("mix", b, 1), i)
                        for g in range(2):
                            ins = nc.vector.scalar_tensor_tensor(out=state[:, b, g], in0=state[:, b, g],
                                                                 scalar=decay_s[:, g:g + 1], in1=upd[:, g],
                                                                 op0=ALU.mult, op1=ALU.add)
                        ins.then_inc(state_done, 1)
                    if stage == "lin":
                        qk_ps, kv_ps = bank(0), bank(1)
                        nc.vector.tensor_scalar(neg_t[:, b], qk_ps[0:MEM, 0:2 * P], 0.0, None, ALU.min)
                        nc.vector.tensor_scalar(neg[:, b], kv_ps[:, 0:MEM], 0.0, None, ALU.min)\
                            .then_inc(neg_done, 1)
                        nc.vector.tensor_copy(v[:, b, 0:MEM], kv_ps[:, MEM:2 * MEM])
                        dve.wait_ge(nexp_done, nth(i, b))
                        frees(nc.vector.scalar_tensor_tensor(
                            out=sig[:, b], in0=qk_ps[0:MEM, 0:2 * P].rearrange("p (a n) -> p a n", a=2), scalar=0.0,
                            in1=neg_t[:, b].rearrange("p (a n) -> p a n", a=2),
                            op0=ALU.max, op1=ALU.add), 0)
                        frees(nc.vector.scalar_tensor_tensor(
                            out=sigk[:, b], in0=kv_ps[:, 0:MEM], scalar=0.0, in1=neg[:, b],
                            op0=ALU.max, op1=ALU.add), 1)
                    if stage == "tri":
                        frees(nc.vector.tensor_tensor(tri[:, b], bank()[:, 0:P], causal[:], ALU.mult))
                    if stage == "num":
                        nu = bank(0)
                        two = nu[:, 0:2 * (MEM + 1)].rearrange("p (a n) -> p a n", a=2)
                        chain(nc.vector.tensor_scalar(den[:, b, 0:2], two[:, :, MEM], CLIP, None, ALU.max))
                        chain(nc.vector.reciprocal(den[:, b, 2:4], den[:, b, 0:2]))
                        chain(nc.vector.tensor_tensor(den[:, b, 4:6], den[:, b, 2:4], mixw[:], ALU.mult))
                        chain(nc.vector.tensor_scalar(comb[:, b], two[:, 0, 0:MEM], den[:, b, 4:5], None, ALU.mult))
                        frees(nc.vector.scalar_tensor_tensor(out=comb[:, b], in0=two[:, 1, 0:MEM],
                                                             scalar=den[:, b, 5:6], in1=comb[:, b],
                                                             op0=ALU.mult, op1=ALU.add), 0)
                        nc.vector.tensor_tensor(state[:, b], state[:, b], bank(1)[0:MEM, 0:MEM + 1], ALU.add)\
                            .then_inc(state_done, 1)
                    if stage == "wo":
                        dve.wait_ge(x_in[b], i * 16 + 16)
                        norm_sums(x[:, b], mv1_done)
                    if stage == "ln1":
                        norm(x1[:, b], rstd1, x1_done)
                    if stage == "sc":
                        for n in range(4):
                            ins = nc.vector.tensor_reduce(peak[:, b % 2, 4 * n:4 * n + 4],
                                                          bank(n)[:, 0:QH].rearrange("p (h k) -> p h k", h=4),
                                                          AX.X, ALU.max)
                        chain(ins)
                        for n in range(4):
                            ins = nc.vector.tensor_tensor(
                                s[:, b % 2, n * QH:(n + 1) * QH].rearrange("p (h k) -> p h k", h=4),
                                bank(n)[:, 0:QH].rearrange("p (h k) -> p h k", h=4),
                                peak[:, b % 2, 4 * n:4 * n + 4].unsqueeze(2).broadcast_to([P, 4, CTX]), ALU.subtract)
                            if n < 3:
                                frees(ins, n)
                        ins.then_inc(s_done, 1)
                    if stage == "pt":
                        for n in (2, 3):
                            frees(nc.vector.tensor_copy(pt[:, b % 2, 4 * n:4 * n + 4],
                                                        bank(n)[0:CTX, :].rearrange("p (h n) -> p h n", h=4)), n)
                    if stage == "pv":
                        o = bank()[:, 0:XH * VW].rearrange("p (h e) -> p h e", e=VW)
                        chain(nc.vector.reciprocal(rsum[:, b], o[:, :, XD]))
                        nc.vector.tensor_tensor(att[:, b].rearrange("p (h e) -> p h e", e=XD), o[:, :, 0:XD],
                                                rsum[:, b].unsqueeze(2).broadcast_to([P, XH, XD]), ALU.mult)\
                            .then_inc(att_done, 1)
                    if stage == "wout":
                        dve.wait_ge(x1b_done, nth(i, b))
                        norm_sums(x1b[:, b], mv2_done)
                    if stage == "ln2":
                        if not first:
                            dve.wait_ge(sent[b], i * 48)
                        norm(x2[:, b], rstd2, x2_done)
                    if stage == "rt":
                        nc.vector.tensor_reduce(nmax[:, b], bank()[:, 0:E], AX.X, ALU.max, negate=True)\
                            .then_inc(nmax_done, 1)
                    if stage == "top":
                        dve.wait_ge(ex_done, nth(i, b))
                        carry(dve, spot[:])
                        chain(nc.vector.max(top8[:, b], ex[:, b]))
                        chain(nc.vector.tensor_reduce(tsum[:, b, 0:1], top8[:, b, 0:top], AX.X, ALU.add))
                        chain(nc.vector.reciprocal(tsum[:, b, 1:2], tsum[:, b, 0:1]))
                        dve.wait_ge(sent[b], i * 48)
                        carry(dve, spot[:])
                        if first:
                            chain(nc.vector.match_replace(rest[:, b], top8[:, b], ex[:, b], -1.0))
                            chain(nc.vector.tensor_scalar(rest[:, b], rest[:, b], 0.0, tsum[:, b, 1:2],
                                                          ALU.is_lt, ALU.mult))
                        else:
                            chain(nc.vector.max_index(top_u[:, b], top8[:, b], ex[:, b]))
                            chain(nc.vector.tensor_copy(top_i[:, b], top_u[:, b]))
                            for k in range(2):
                                chain(nc.vector.tensor_scalar(hot[:, b, k], iota[:], top_i[:, b, k:k + 1],
                                                              tsum[:, b, 1:2], ALU.is_equal, ALU.mult))
                            chain(nc.vector.tensor_tensor(rest[:, b], hot[:, b, 0], hot[:, b, 1], ALU.add))
                        nc.vector.tensor_tensor(cw[:, b], rest[:, b], ex[:, b], ALU.mult).then_inc(cw_done, 1)
                    if stage == "b2":
                        dve.wait_ge(x2s_done, nth(i, b))
                        dve.wait_ge(sent[b], i * 48)
                        nc.vector.tensor_tensor(xr[:, b], bank()[:, 0:DM], x1b[:, b], ALU.add).then_inc(xr_done, 1)

        @block.tensor
        def _(pe):
            mm, tr = nc.tensor.matmul, nc.tensor.transpose
            pe.wait_ge(consts, 16 * len(loads))
            if not first:
                for b in range(NB):
                    for g in range(KC):
                        for c in range(KC):
                            ins = mm(psum[2 * b][:, g * CTX:(g + 1) * CTX], wk[:, c, g * P:(g + 1) * P],
                                     ctx_t[:, b, c], start=c == 0, stop=c == KC - 1)
                    ins.then_inc(prep_pe, 1)
                    for c in range(KC):
                        ins = mm(psum[2 * b + 1][0:CTX, 0:DM], ctx_t[:, b, c], wv[:, c],
                                 start=c == 0, stop=c == KC - 1)
                    ins.then_inc(prep_pe, 1)
            else:
                pe.wait_ge(prep_pool, 3)
            pe.wait_ge(prep, VPREP[layer])
            with pe.Fori(0, STEPS) as i:
                for stage, b in order:
                    def bank(n=0, stage=stage, b=b):
                        k, use = plan.place[(stage, b, n)]
                        if use:
                            freed(pe, by_place[(k, use - 1)], i)
                        else:
                            freed_before(pe, k, i)
                        return psum[k]

                    def fills(ins, n=0, stage=stage, b=b):
                        ins.then_inc(full[plan.bank((stage, b, n))], 1)

                    if stage == "qkv":
                        pe.wait_ge(xt_in[b], i * 16 + 16)
                        out = bank(0)
                        for a in range(4):
                            for c in range(KC):
                                ins = mm(out[:, a * P:(a + 1) * P], wqk[:, c, a * P:(a + 1) * P], xt[:, b, c],
                                         start=c == 0, stop=c == KC - 1)
                        fills(ins, 0)
                        out = bank(1)
                        for c in range(KC):
                            ins = mm(out[:], xt[:, b, c], wkv[:, c], start=c == 0, stop=c == KC - 1)
                        fills(ins, 1)
                    if stage == "ret":
                        pe.wait_ge(moved, nth(i, b))
                        outs = [bank(r) for r in range(4)]
                        for g in range(2):
                            for r in range(4):
                                rows = slice(RD * r, RD * (r + 1))
                                ins = mm(outs[r][:, g * P:(g + 1) * P], qk[rows, b, 2 + g], qk[rows, b, g],
                                         start=True, stop=True)
                                if g == 1:
                                    fills(ins, r)
                    if stage == "mix":
                        pe.wait_ge(qkd_done, nth(i, b))
                        pe.wait_ge(state_done, nth(i, b))
                        out = bank(0)
                        for g in range(2):
                            mm(out[:, g * P:(g + 1) * P], state[:, b, g], qd[:, b, g], start=g == 0, stop=False,
                               skip_group_check=True)
                        for n in range(4):
                            freed(pe, ("ret", b, n), i)
                        for g in range(2):
                            for r in range(4):
                                h = 4 * g + r
                                ins = mm(out[RD * r:RD * (r + 1), g * P:(g + 1) * P], v[:, b, h * RD:(h + 1) * RD],
                                         prob[:, b % 2, r, g], start=False, stop=True, skip_group_check=True)
                        fills(ins, 0)
                        out = bank(1)
                        for g in range(2):
                            ins = mm(out[:, g * P:(g + 1) * P], kd[:, b, g * P:(g + 1) * P],
                                     v[:, b, g * P:(g + 1) * P], start=True, stop=True)
                        fills(ins, 1)
                    if stage == "x0t":
                        pe.wait_ge(x_in[b], i * 16 + 16)
                        out = bank()
                        for c in range(KC):
                            ins = tr(out[:, c * P:(c + 1) * P], x[:, b, c * P:(c + 1) * P], ident[:])
                        fills(ins)
                    if stage == "lin":
                        pe.wait_ge(moved, nth(i, b))
                        out = bank(0)
                        for a in range(2):
                            for c in range(KC):
                                ins = mm(out[0:MEM, a * P:(a + 1) * P], wqk[:, c, a * MEM:(a + 1) * MEM], xt[:, b, c],
                                         start=c == 0, stop=c == KC - 1)
                        fills(ins, 0)
                        out = bank(1)
                        for c in range(KC):
                            ins = mm(out[:, 0:2 * MEM], xt[:, b, c], wkv[:, c], start=c == 0, stop=c == KC - 1)
                        fills(ins, 1)
                    if stage == "tri":
                        freed(pe, ("lin", b, 0), i)
                        fills(mm(bank()[:, 0:P], sig[:, b, 1], sig[:, b, 0], start=True, stop=True))
                    if stage == "num":
                        freed(pe, ("tri", b, 0), i)
                        freed(pe, ("lin", b, 1), i)
                        pe.wait_ge(state_done, nth(i, b))
                        out = bank(0)
                        mm(out[:, MEM + 1:2 * (MEM + 1)], sig[:, b, 0], memory[:], start=True, stop=True)
                        mm(out[:, 0:MEM + 1], sig[:, b, 0], state[:, b], start=True, stop=False)
                        fills(mm(out[:, 0:MEM + 1], tri[:, b], v[:, b], start=False, stop=True), 0)
                        fills(mm(bank(1)[0:MEM, 0:MEM + 1], sigk[:, b], v[:, b], start=True, stop=True), 1)
                    if stage == "ct":
                        freed(pe, ("num", b, 0), i)
                        out = bank()
                        fills(mm(out[0:MEM, 0:P], comb[:, b], ident[:], start=True, stop=True))
                    if stage == "wo":
                        out = bank()
                        if first:
                            pe.wait_ge(o_moved, nth(i, b))
                            for c in range(KC):
                                ins = mm(out[:, 0:DM], ot[:, b, c], wo[:, c], start=c == 0, stop=c == KC - 1)
                        else:
                            pe.wait_ge(combt_done, nth(i, b))
                            ins = mm(out[:, 0:DM], combt[:, b], wo[:], start=True, stop=True)
                        fills(ins)
                    if stage in ("x1t", "at", "x2t"):
                        ready, rows = {"x1t": (x1_done, x1), "at": (att_done, att), "x2t": (x2_done, x2)}[stage]
                        pe.wait_ge(ready, nth(i, b))
                        out = bank()
                        for c in range(KC):
                            ins = tr(out[:, c * P:(c + 1) * P], rows[:, b, c * P:(c + 1) * P], ident[:])
                        fills(ins)
                    if stage == "q":
                        pe.wait_ge(x1t_done, nth(i, b))
                        out = bank()
                        for g in range(KC):
                            for c in range(KC):
                                ins = mm(out[:, g * P:(g + 1) * P], wq[:, c, g * P:(g + 1) * P], x1t[:, b, c],
                                         start=c == 0, stop=c == KC - 1)
                        fills(ins)
                    if stage == "sc":
                        pe.wait_ge(x1t_done if first else q_done, nth(i, b))
                        for n in range(4):
                            g = n // 2
                            fills(mm(bank(n)[:, 0:QH], (x1t if first else qt)[:, b, g],
                                     keys[:, b, g, (n % 2) * QH:(n % 2 + 1) * QH], start=True, stop=True), n)
                    if stage == "pt":
                        pe.wait_ge(exp_done, nth(i, b))
                        for n in range(4):
                            out = bank(n)
                            for j in range(4):
                                h = 4 * n + j
                                ins = tr(out[0:CTX, j * P:(j + 1) * P], s[:, b % 2, h * CTX:(h + 1) * CTX], ident[:])
                            fills(ins, n)
                    if stage == "pv":
                        pe.wait_ge(pta_done, 2 * nth(i, b))
                        freed(pe, ("pt", b, 2), i)
                        freed(pe, ("pt", b, 3), i)
                        out = bank()
                        for h in range(XH):
                            ins = mm(out[:, h * VW:(h + 1) * VW], pt[:, b % 2, h], vals[:, b, h],
                                     start=True, stop=True)
                        fills(ins)
                    if stage == "wout":
                        pe.wait_ge(att_t_done, nth(i, b))
                        out = bank()
                        for c in range(KC):
                            ins = mm(out[:, 0:DM], att_t[:, b, c], wout[:, c], start=c == 0, stop=c == KC - 1)
                        fills(ins)
                    if stage == "rt":
                        pe.wait_ge(x2t_done, nth(i, b))
                        out = bank()
                        for c in range(KC):
                            ins = mm(out[:, 0:E], x2t[:, b, c], router[:, c], start=c == 0,
                                     stop=c == KC - 1 and not first)
                        if first:
                            ins = mm(out[:, 0:E], ones[:], router_b[:], start=False, stop=True)
                        fills(ins)
                    if stage == "cwt":
                        pe.wait_ge(cw_done, nth(i, b))
                        out = bank()
                        fills(mm(out[0:E, 0:P], cw[:, b], ident[:], start=True, stop=True))
                    if stage == "b2":
                        pe.wait_ge(cwt_done, nth(i, b))
                        fills(mm(bank()[:, 0:DM], cwt[:, b], b2[:], start=True, stop=True))


TOK = 512
SUB = TOK // P
TILES = NT // TOK
E0, H0, HS, ES = 64, 64, 512, 2
E1, H1 = 8, 512


def shared_routed_phase(nc, sems, d, w1, w2, w_in, src, src_t, src_cw, dst):
    PAIRS, CH = E0 // 2, ES * HS // P
    UNITS = CH + PAIRS
    JOBS = SUB + PAIRS * 2 * SUB
    with ExitStack() as ctx:
        def sb(name, shape):
            return ctx.enter_context(nc.sbuf_tensor(f"b_{name}", shape, F32))

        def sem(name):
            return sems.enter_context(nc.semaphore(f"b_{name}"))

        hp = [ctx.enter_context(nc.psum_tensor(f"b_hp{k}", [P, 512], F32)) for k in range(4)]
        yp = [ctx.enter_context(nc.psum_tensor(f"b_yp{k}", [P, 512], F32)) for k in range(4)]
        sw1 = sb("sw1", [P, KC, ES * HS])
        sw2 = sb("sw2", [P, CH, DM])
        b1 = sb("b1", [P, PAIRS])
        sb1 = sb("sb1", [P, CH])
        half = sb("half", [P, 1])
        eps = sb("eps", [P, 1])
        spot = sb("spot", [P, 1])
        xt = sb("xt", [P, 2, KC, TOK])
        xr = sb("xr", [P, 2, SUB, DM])
        cw = sb("cw", [P, 2, SUB, E0])
        h = sb("h", [P, 4, TOK])
        acc = sb("acc", [P, 2, SUB, DM])
        stats = sb("stats", [P, SUB, 6])
        mv = sb("mv", [P, SUB, 4])
        out = sb("out", [P, SUB, DM])

        consts = sem("consts")
        xt_in = [sem(f"xt_in{k}") for k in range(2)]
        row_in = [sem(f"row_in{k}") for k in range(2)]
        rows_used = sem("rows_used")
        h_full = sem("h_full")
        h_done = sem("h_done")
        h_used = sem("h_used")
        y_full = sem("y_full")
        y_used = sem("y_used")
        z_done = sem("z_done")
        st_done = sem("st_done")
        mv_done = sem("mv_done")
        ve_done = sem("ve_done")
        rstd = sem("rstd")
        out_done = sem("out_done")
        sent = sem("sent")
        half_done = sem("half_done")

        loads = [(sw1[:, :, e * HS:(e + 1) * HS], d["sw1"][e].rearrange("(c p) n -> p c n", p=P)) for e in range(ES)]
        loads += [(sw2[:], d["sw2"].rearrange("e (c p) n -> p (e c) n", p=P)), (b1[:], d["b1"]), (sb1[:], d["sb1"])]
        block = ctx.enter_context(nc.Block())

        @block.sync
        def _(sp):
            def load(k, span):
                sp.dma_start(xt[:, k], src_t[:, span].rearrange("(c p) n -> p c n", p=P)).then_inc(xt_in[k], 16)
                sp.dma_start(xr[:, k], src[span, :].rearrange("(t p) n -> p t n", p=P)).then_inc(row_in[k], 16)
                sp.dma_start(cw[:, k], src_cw[span, :].rearrange("(t p) n -> p t n", p=P)).then_inc(row_in[k], 16)

            load(0, slice(0, TOK))
            for a, b in loads:
                sp.dma_start(a, b).then_inc(consts, 16)
            load(1, slice(TOK, 2 * TOK))
            with sp.Fori(1, TILES // 2) as i:
                for k in range(2):
                    T = 2 * i + k
                    sp.wait_ge(h_full, (T - 1) * UNITS)
                    sp.wait_ge(rows_used, T - 1)
                    load(k, bass.ds(T * TOK, TOK))

        @block.gpsimd
        def _(pool):
            nc.gpsimd.memset(half[:], -0.5)
            nc.gpsimd.memset(eps[:], LN_EPS).then_inc(half_done, 1)
            pool.wait_ge(half_done, 1)
            with pool.Fori(0, TILES) as T:
                pool.wait_ge(mv_done, T + 1)
                nc.gpsimd.tensor_tensor(mv[:, :, 2], mv[:, :, 1], eps[:].broadcast_to([P, SUB]), ALU.add).then_inc(ve_done, 1)
                pool.wait_ge(ve_done, T + 1)
                nc.gpsimd.tensor_tensor(mv[:, :, 3], mv[:, :, 2], half[:].broadcast_to([P, SUB]), ALU.pow)\
                    .then_inc(rstd, 1)
                pool.wait_ge(out_done, T + 1)
                pool.dma_start(dst[bass.ds(T * TOK, TOK), :].rearrange("(t p) n -> p t n", p=P), out[:])\
                    .then_inc(sent, 16)
            pool.wait_ge(sent, 16 * TILES)

        def multiplied(eng, T, u):
            if u < 0:
                eng.wait_ge(y_full, T * JOBS)
            elif u < CH - 1:
                eng.wait_ge(h_used, T * (CH - 1) + u + 1)
            else:
                eng.wait_ge(y_full, T * JOBS + SUB + (u - CH + 1) * 2 * SUB)

        @block.scalar
        def _(act):
            act.wait_ge(consts, 16 * len(loads))
            with act.Fori(0, TILES) as T:
                for u in range(UNITS):
                    act.wait_ge(h_full, T * UNITS + u + 1)
                    multiplied(act, T, u - 4)
                    bias = sb1[:, u:u + 1] if u < CH else b1[:, u - CH:u - CH + 1]
                    nc.scalar.activation(h[:, u % 4], hp[u % 4][:], ACT.Silu, bias=bias).then_inc(h_done, 1)

        @block.vector
        def _(dve):
            with dve.Fori(0, TILES // 2) as i:
                for k in range(2):
                    T = 2 * i + k
                    dve.wait_ge(row_in[k], 32 * i + 32)
                    dve.wait_ge(out_done, T)
                    for j in range(JOBS):
                        y = yp[j % 4][:, 0:DM]
                        dve.wait_ge(y_full, T * JOBS + j + 1)
                        if j < SUB:
                            ins = nc.vector.tensor_tensor(acc[:, 0, j], y, xr[:, k, j], ALU.add)
                        else:
                            p, t, e = (j - SUB) // 8, (j - SUB) % 8 // 2, j % 2
                            w = cw[:, k, t, 2 * p + e:2 * p + e + 1]
                            if e == 0 or p > 0:
                                dve.wait_ge(y_used, T * JOBS + (t if p == 0 else j - 8) + 1)
                                ins = nc.vector.scalar_tensor_tensor(out=acc[:, e, t], in0=y, scalar=w,
                                                                     in1=acc[:, e, t], op0=ALU.mult, op1=ALU.add)
                            else:
                                ins = nc.vector.tensor_scalar(acc[:, e, t], y, w, None, ALU.mult)
                        ins.then_inc(y_used, 1)
                    dve.wait_ge(y_used, (T + 1) * JOBS)
                    nc.vector.tensor_tensor(acc[:, 0], acc[:, 0], acc[:, 1], ALU.add).then_inc(rows_used, 1)
                    dve.wait_ge(rows_used, T + 1)
                    for t in range(SUB):
                        ins = nc.vector.bn_stats(stats[:, t], acc[:, 0, t])
                    ins.then_inc(st_done, 1)
                    dve.wait_ge(st_done, T + 1)
                    carry(dve, spot[:])
                    for t in range(SUB):
                        ins = nc.vector.bn_aggr(mv[:, t, 0:2], stats[:, t])
                    ins.then_inc(mv_done, 1)
                    dve.wait_ge(rstd, T + 1)
                    dve.wait_ge(sent, T * 16)
                    for t in range(SUB):
                        ins = nc.vector.tensor_scalar(out[:, t], acc[:, 0, t], mv[:, t, 0:1], mv[:, t, 3:4],
                                                      ALU.subtract, ALU.mult)
                    ins.then_inc(out_done, 1)

        @block.tensor
        def _(pe):
            mm = nc.tensor.matmul
            pe.wait_ge(consts, 16 * len(loads))
            pe.wait_ge(w_in, 32)

            def hidden(T, k, u):
                pe.wait_ge(h_done, T * UNITS + max(0, u - 3))
                for c in range(KC):
                    w = sw1[:, c, u * P:(u + 1) * P] if u < CH else w1[:, c, (u - CH) * P:(u - CH + 1) * P]
                    ins = mm(hp[u % 4][:], w, xt[:, k, c], start=c == 0, stop=c == KC - 1)
                ins.then_inc(h_full, 1)

            def outward(T, u):
                pe.wait_ge(h_done, T * UNITS + u + 1)
                if u < CH:
                    if u == 0:
                        pe.wait_ge(y_used, T * JOBS)
                    for t in range(SUB):
                        ins = mm(yp[t][:, 0:DM], h[:, u % 4, t * P:(t + 1) * P], sw2[:, u], start=u == 0,
                                 stop=u == CH - 1)
                        if u == CH - 1:
                            ins.then_inc(y_full, 1)
                    if u < CH - 1:
                        ins.then_inc(h_used, 1)
                else:
                    for t in range(SUB):
                        for e in range(2):
                            j = SUB + (u - CH) * 8 + 2 * t + e
                            pe.wait_ge(y_used, T * JOBS + j - 3)
                            rows = slice(H0 * e, H0 * (e + 1))
                            mm(yp[j % 4][:, 0:DM], h[rows, u % 4, t * P:(t + 1) * P], w2[rows, u - CH],
                               start=True, stop=True).then_inc(y_full, 1)

            with pe.Fori(0, TILES // 2) as i:
                for k in range(2):
                    T = 2 * i + k
                    pe.wait_ge(xt_in[k], 16 * i + 16)
                    for u in range(UNITS):
                        hidden(T, k, u)
                        if u:
                            outward(T, u - 1)
                    outward(T, UNITS - 1)


def gated_phase(nc, sems, d, wg, wu, w_in, src, src_t, src_cw, out_rows):
    HC = H1 // P
    UNITS = E1 * HC
    JOBS = E1 * SUB
    with ExitStack() as ctx:
        def sb(name, shape):
            return ctx.enter_context(nc.sbuf_tensor(f"d_{name}", shape, F32))

        def sem(name):
            return sems.enter_context(nc.semaphore(f"d_{name}"))

        hp = [ctx.enter_context(nc.psum_tensor(f"d_hp{k}", [P, 512], F32)) for k in range(4)]
        yp = [ctx.enter_context(nc.psum_tensor(f"d_yp{k}", [P, 512], F32)) for k in range(4)]
        wd = sb("wd", [P, E1 * HC, DM])
        half = sb("half", [P, 1])
        eps = sb("eps", [P, 1])
        spot = sb("spot", [P, 1])
        xt = sb("xt", [P, 2, KC, TOK])
        xr = sb("xr", [P, 2, SUB, DM])
        cw = sb("cw", [P, 2, SUB, E1])
        gate = sb("gate", [P, 2, TOK])
        h = sb("h", [P, 2, HC, TOK])
        acc = sb("acc", [P, SUB, DM])
        stats = sb("stats", [P, SUB, 6])
        mv = sb("mv", [P, SUB, 4])
        out = sb("out", [P, SUB, DM])

        consts = sem("consts")
        xt_in = [sem(f"xt_in{k}") for k in range(2)]
        row_in = [sem(f"row_in{k}") for k in range(2)]
        g_full = sem("g_full")
        u_full = sem("u_full")
        g_done = sem("g_done")
        h_done = sem("h_done")
        y_full = sem("y_full")
        y_used = sem("y_used")
        st_done = sem("st_done")
        mv_done = sem("mv_done")
        ve_done = sem("ve_done")
        rstd = sem("rstd")
        out_done = sem("out_done")
        sent = sem("sent")
        half_done = sem("half_done")
        block = ctx.enter_context(nc.Block())

        @block.sync
        def _(sp):
            def load(k, span):
                sp.dma_start(xt[:, k], src_t[:, span].rearrange("(c p) n -> p c n", p=P)).then_inc(xt_in[k], 16)
                sp.dma_start(xr[:, k], src[span, :].rearrange("(t p) n -> p t n", p=P)).then_inc(row_in[k], 16)
                sp.dma_start(cw[:, k], src_cw[span, :].rearrange("(t p) n -> p t n", p=P)).then_inc(row_in[k], 16)

            load(0, slice(0, TOK))
            sp.dma_start(wd[:], d["wd"].rearrange("(c p) n -> p c n", p=P)).then_inc(consts, 16)
            load(1, slice(TOK, 2 * TOK))
            with sp.Fori(1, TILES // 2) as i:
                for k in range(2):
                    T = 2 * i + k
                    sp.wait_ge(u_full, (T - 1) * UNITS)
                    sp.wait_ge(st_done, T - 1)
                    load(k, bass.ds(T * TOK, TOK))

        @block.gpsimd
        def _(pool):
            nc.gpsimd.memset(half[:], -0.5)
            nc.gpsimd.memset(eps[:], LN_EPS).then_inc(half_done, 1)
            pool.wait_ge(half_done, 1)
            with pool.Fori(0, TILES) as T:
                pool.wait_ge(mv_done, T + 1)
                nc.gpsimd.tensor_tensor(mv[:, :, 2], mv[:, :, 1], eps[:].broadcast_to([P, SUB]), ALU.add).then_inc(ve_done, 1)
                pool.wait_ge(ve_done, T + 1)
                nc.gpsimd.tensor_tensor(mv[:, :, 3], mv[:, :, 2], half[:].broadcast_to([P, SUB]), ALU.pow)\
                    .then_inc(rstd, 1)
                pool.wait_ge(out_done, T + 1)
                pool.dma_start(out_rows[bass.ds(T * TOK, TOK), :].rearrange("(t p) n -> p t n", p=P), out[:])\
                    .then_inc(sent, 16)
            pool.wait_ge(sent, 16 * TILES)

        @block.scalar
        def _(act):
            with act.Fori(0, TILES) as T:
                for u in range(UNITS):
                    act.wait_ge(g_full, T * UNITS + u + 1)
                    act.wait_ge(h_done, T * UNITS + max(0, u - 1))
                    nc.scalar.activation(gate[:, u % 2], hp[2 * (u % 2)][:], ACT.Silu).then_inc(g_done, 1)

        @block.vector
        def _(dve):
            with dve.Fori(0, TILES // 2) as i:
                for k in range(2):
                    T = 2 * i + k
                    dve.wait_ge(row_in[k], 32 * i + 32)
                    dve.wait_ge(out_done, T)

                    def hidden(u):
                        e, c = u // HC, u % HC
                        dve.wait_ge(u_full, T * UNITS + u + 1)
                        dve.wait_ge(g_done, T * UNITS + u + 1)
                        dve.wait_ge(y_full, T * JOBS + max(0, e - 1) * SUB)
                        nc.vector.tensor_tensor(h[:, e % 2, c], gate[:, u % 2], hp[2 * (u % 2) + 1][:], ALU.mult)\
                            .then_inc(h_done, 1)

                    def gather(e, t):
                        j = e * SUB + t
                        dve.wait_ge(y_full, T * JOBS + j + 1)
                        if e:
                            dve.wait_ge(y_used, T * JOBS + j - SUB + 1)
                        nc.vector.scalar_tensor_tensor(out=acc[:, t], in0=yp[t][:, 0:DM], scalar=cw[:, k, t, e:e + 1],
                                                       in1=acc[:, t] if e else xr[:, k, t], op0=ALU.mult,
                                                       op1=ALU.add).then_inc(y_used, 1)

                    for u in range(UNITS):
                        hidden(u)
                        if u >= HC:
                            gather(u // HC - 1, u % HC)
                    for t in range(SUB):
                        gather(E1 - 1, t)
                    for t in range(SUB):
                        dve.wait_ge(y_used, (T + 1) * JOBS - SUB + 1 + t)
                        ins = nc.vector.bn_stats(stats[:, t], acc[:, t])
                    ins.then_inc(st_done, 1)
                    dve.wait_ge(st_done, T + 1)
                    carry(dve, spot[:])
                    for t in range(SUB):
                        ins = nc.vector.bn_aggr(mv[:, t, 0:2], stats[:, t])
                    ins.then_inc(mv_done, 1)
                    dve.wait_ge(rstd, T + 1)
                    dve.wait_ge(sent, T * 16)
                    for t in range(SUB):
                        ins = nc.vector.tensor_scalar(out[:, t], acc[:, t], mv[:, t, 0:1], mv[:, t, 3:4],
                                                      ALU.subtract, ALU.mult)
                    ins.then_inc(out_done, 1)

        @block.tensor
        def _(pe):
            mm = nc.tensor.matmul
            pe.wait_ge(consts, 16)
            pe.wait_ge(w_in, 64)
            with pe.Fori(0, TILES // 2) as i:
                for k in range(2):
                    T = 2 * i + k
                    pe.wait_ge(xt_in[k], 16 * i + 16)

                    def outward(e, t):
                        pe.wait_ge(h_done, T * UNITS + (e + 1) * HC)
                        pe.wait_ge(y_used, T * JOBS + max(0, (e - 1) * SUB + t + 1))
                        for c in range(HC):
                            ins = mm(yp[t][:, 0:DM], h[:, e % 2, c, t * P:(t + 1) * P], wd[:, e * HC + c],
                                     start=c == 0, stop=c == HC - 1)
                        ins.then_inc(y_full, 1)

                    for u in range(UNITS):
                        pe.wait_ge(h_done, T * UNITS + max(0, u - 1))
                        for which, w, full in ((0, wg, g_full), (1, wu, u_full)):
                            for c in range(KC):
                                ins = mm(hp[2 * (u % 2) + which][:], w[:, c, u * P:(u + 1) * P], xt[:, k, c],
                                         start=c == 0, stop=c == KC - 1)
                            ins.then_inc(full, 1)
                        if u >= HC:
                            outward(u // HC - 1, u % HC)
                    for t in range(SUB):
                        outward(E1 - 1, t)


def decoder(nc, a, out):
    def scratch(name, shape):
        return nc.dram_tensor(name, shape, F32, kind="Internal").ap()

    res1, res1_t, cw1 = scratch("res1", [NT, DM]), scratch("res1_t", [DM, NT]), scratch("cw1", [NT, E0])
    mid = scratch("mid", [NT, DM])
    res2, res2_t, cw2 = scratch("res2", [NT, DM]), scratch("res2_t", [DM, NT]), scratch("cw2", [NT, E1])
    layer0 = {k: a[k] for k in ("ident", "head_mask", "ctx_t", "ctx", "decay", "decay_q", "decay_k", "decay_s",
                                "block_mask")}
    layer0.update(wq=a["L0_wq"], wk=a["L0_wk"], wv=a["L0_wv"], wo=a["L0_wo"], wout=a["L0_wout"], bout=a["L0_bout"],
                  router=a["L0_router"], router_b=a["L0_router_b"], b2=a["L0_b2"], sb2=a["L0_sb2"])
    layer1 = {k: a[k] for k in ("ident", "head_mask", "ctx_t", "causal", "iota")}
    layer1.update(wq1=a["L1_mq"], wk1=a["L1_mk"], wv1=a["L1_mv"], wo1=a["L1_mo"], gate=a["L1_gate"],
                  memory=a["L1_memory"], mem_norm=a["L1_norm"], mem_norm_rows=a["L1_norm_rows"],
                  wq=a["L1_wq"], wk=a["L1_wk"], wv=a["L1_wv"], wout=a["L1_wout"], bout=a["L1_bout"],
                  router=a["L1_router"])
    with ExitStack() as ctx:
        big = ctx.enter_context(nc.sbuf_tensor("big", [P, 4 * 4096 + 5120], F32))
        sems = ctx.enter_context(ExitStack())
        w_in = ctx.enter_context(nc.semaphore("w_in"))
        halves = [big[:, n * 8192:(n + 1) * 8192] for n in range(2)]
        spare = big[:, 16384:]
        as_cols = [t.rearrange("p (c n) -> p c n", c=KC) for t in halves]
        w2 = halves[1].rearrange("p (c n) -> p c n", n=DM)

        def load_layer0(sp):
            sp.dma_start(as_cols[0], a["L0_w1"].rearrange("(c p) n -> p c n", p=P)).then_inc(w_in, 16)
            sp.dma_start(w2, a["L0_w2"].rearrange("(c p) n -> p c n", p=P)).then_inc(w_in, 16)

        def load_layer1(sp):
            for t, name in zip(as_cols, ("L1_wg", "L1_wu")):
                sp.dma_start(t, a[name].rearrange("(c p) n -> p c n", p=P)).then_inc(w_in, 16)

        attention_phase(nc, sems, 0, layer0, a["x"], a["x_t"], res1, res1_t, cw1, E0, 8, load_layer0, spare)
        shared_routed_phase(nc, sems, dict(sw1=a["L0_sw1"], sw2=a["L0_sw2"], b1=a["L0_b1"], sb1=a["L0_sb1"]),
                            as_cols[0], w2, w_in, res1, res1_t, cw1, mid)
        attention_phase(nc, sems, 1, layer1, mid.rearrange("(b s) n -> b s n", b=NB), None, res2, res2_t, cw2, E1, 2,
                        load_layer1, spare)
        gated_phase(nc, sems, dict(wd=a["L1_wd"]), as_cols[0], as_cols[1], w_in, res2, res2_t, cw2, out)


def shape_constants():
    gamma = 1.0 - 2.0 ** (-5.0 - np.arange(RH))
    at = np.arange(P)
    diff = at[None, :] - at[:, None]
    table = np.where(diff >= 0, gamma[:, None, None] ** np.maximum(diff, 0), 0.0) * RD ** -0.5
    return {
        "ident": np.eye(P),
        "head_mask": at[:, None] // XD == np.arange(P // XD)[None, :],
        "decay": table.reshape(2, 4, P, P).transpose(2, 1, 0, 3),
        "decay_q": (np.repeat(gamma, RD)[:, None] ** (at[None, :] + 1) * RD ** -0.5).reshape(2, P, P)
        .transpose(1, 0, 2),
        "decay_k": np.repeat(gamma, RD)[None, :] ** (P - 1 - at[:, None]),
        "decay_s": (np.repeat(gamma, RD) ** P).reshape(2, P).T,
        "block_mask": at[:, None] // RD == at[None, :] // RD,
        "causal": diff >= 0,
        "iota": np.broadcast_to(np.arange(E1), (P, E1)),
    }


def kernel(**inputs):
    import concourse.bacc as _bacc
    from concourse.bass_utils import run_bass_kernel_spmd as _run

    t = {k: np.asarray(v) for k, v in inputs.items()}
    laid = {
        "x": t["x"], "x_t": t["x"].transpose(0, 2, 1), "ctx": t["ctx_1024"], "ctx_t": t["ctx_1024"].transpose(0, 2, 1),
        "L0_wq": t["L0_attn_Wq"], "L0_wk": t["L0_attn_Wk"], "L0_wv": t["L0_attn_Wv"], "L0_wo": t["L0_attn_Wo"],
        "L0_wout": t["L0_xattn_W_out"].T, "L0_bout": np.broadcast_to(t["L0_xattn_b_out"], (P, DM)),
        "L0_router": t["L0_ffn_router_w"], "L0_router_b": t["L0_ffn_router_b"].reshape(1, E0),
        "L0_w1": t["L0_ffn_w1"].transpose(1, 0, 2).reshape(DM, E0 * H0),
        "L0_b1": t["L0_ffn_b1"].reshape(E0 // 2, P).T,
        "L0_w2": t["L0_ffn_w2"].reshape(E0 * H0, DM), "L0_b2": t["L0_ffn_b2"],
        "L0_sw1": t["L0_ffn_sw1"], "L0_sb1": t["L0_ffn_sb1"].reshape(ES * HS // P, P).T,
        "L0_sw2": t["L0_ffn_sw2"], "L0_sb2": np.broadcast_to(t["L0_ffn_sb2"], (P, ES, DM)),
        "L1_mq": t["L1_attn_w_q"].T, "L1_mk": t["L1_attn_w_k"].T, "L1_mv": t["L1_attn_w_v"].T,
        "L1_mo": t["L1_attn_w_o"].T, "L1_gate": np.broadcast_to(t["L1_attn_gate"], (P, 1)),
        "L1_memory": t["L1_attn_memory"], "L1_norm": t["L1_attn_memory_norm"].reshape(MEM, 1),
        "L1_norm_rows": np.broadcast_to(t["L1_attn_memory_norm"], (P, MEM)),
        "L1_wq": t["L1_xattn_W_q"], "L1_wk": t["L1_xattn_W_k"], "L1_wv": t["L1_xattn_W_v"],
        "L1_wout": t["L1_xattn_W_o"], "L1_bout": np.broadcast_to(t["L1_xattn_b_o"], (P, DM)),
        "L1_router": t["L1_ffn_router_w"].T,
        "L1_wg": t["L1_ffn_w_gate"].transpose(2, 0, 1).reshape(DM, E1 * H1),
        "L1_wu": t["L1_ffn_w_up"].transpose(2, 0, 1).reshape(DM, E1 * H1),
        "L1_wd": t["L1_ffn_w_down"].transpose(0, 2, 1).reshape(E1 * H1, DM),
    }
    laid.update({k: v.astype(np.float32) for k, v in shape_constants().items()})
    nc = _bacc.Bacc("TRN2", target_bir_lowering=False, num_devices=1)
    arrays, aps = {}, {}
    for name, array in laid.items():
        arrays[f"in_{name}"] = np.ascontiguousarray(array)
        aps[name] = nc.dram_tensor(f"in_{name}", array.shape, F32, kind="ExternalInput").ap()
    out = nc.dram_tensor("out", (NT, DM), F32, kind="ExternalOutput").ap()
    decoder(nc, aps, out)
    r = _run(nc, [arrays], core_ids=[0])
    return r.results[0]["out"].reshape(NB, SEQ, DM)
```

```python
from contextlib import ExitStack

import numpy as np
import concourse.bass as bass
from concourse import mybir

F32 = mybir.dt.float32
ALU = mybir.AluOpType
ACT = mybir.ActivationFunctionType
AX = mybir.AxisListType

P = 128
NB, SEQ, DM = 4, 1024, 256
NT = NB * SEQ
KC = DM // P
CTX = 77
XH, XD = 16, 16
VW = XD + 1
QH = 4 * CTX
RH, RD = 8, 32
MEM = 64
STEPS = SEQ // P
LN_EPS = 1e-5
CLIP = 1e-6
E0, H0, HS, ES = 64, 64, 512, 2
E1, H1, K1 = 8, 512, 2
CAP = NT + P
ROWS1 = NT * K1 // P + E1
ROW = DM + 4


class BankPlan:

    def __init__(self, jobs, banks, uses_before=None):
        self.banks = banks
        self.place, self.uses = {}, {k: 0 for k in banks}
        for n, job in enumerate(jobs):
            k = banks[n % len(banks)]
            self.place[job] = (k, self.uses[k])
            self.uses[k] += 1

    def bank(self, job):
        return self.place[job][0]

    def before(self, job, i):
        k, n = self.place[job]
        return i * self.uses[k] + n

    def after(self, job, i):
        return self.before(job, i) + 1


class Chain:

    def __init__(self, eng, sem, per_pass):
        self.eng, self.sem, self.n, self.count, self.base = eng, sem, per_pass, 0, 0

    def start(self, i):
        assert self.count in (0, self.n), (self.count, self.n)
        self.base, self.count = i * self.n, 0

    def __call__(self, ins, carrier=None):
        self.count += 1
        ins.then_inc(self.sem, 1)
        self.eng.wait_ge(self.sem, self.base + self.count)
        if carrier is not None:
            carry(self.eng, carrier)


def carry(dve, spot):
    dve.memset(spot, 0.0)


def take(nc, sems, name):
    sems.append(nc.alloc_semaphore(name))
    return sems[-1]


def carry_pool(pool, spot):
    return pool.tensor_tensor(spot[:, 1:2], spot[:, 0:1], spot[:, 0:1], ALU.add)


def wavefront(groups):
    order = []
    for group in groups:
        for step in range(NB + len(group) - 1):
            for k, stage in enumerate(group):
                if 0 <= step - k < NB:
                    order.append((stage, step - k))
    return order


VCHAIN = {0: 36, 1: 76}
VPREP = {0: 12, 1: 26}


def attention_phase(nc, sems, layer, d, src, src_t, dst, dst_t, dst_cw, experts, top, prefetch, spare,
                    lists=None, listed=None):
    first = layer == 0
    if first:
        groups = [["qkv"], ["ret", "mix"], ["wo"], ["ln1"], ["x1t"], ["sc", "pt", "pv"], ["at"], ["wout"],
                  ["ln2"], ["x2t"], ["rt"], ["top"], ["cwt"], ["b2"]]
        banks_of = {"qkv": 2, "ret": 4, "mix": 2, "wo": 1, "x1t": 1, "sc": 4, "pt": 4, "pv": 1, "at": 1,
                    "wout": 1, "x2t": 1, "rt": 1, "cwt": 1, "b2": 1}
    else:
        groups = [["x0t"], ["lin"], ["tri"], ["num"], ["ct"], ["wo"], ["ln1"], ["x1t"], ["q"],
                  ["sc", "pt", "pv"], ["at"], ["wout"], ["ln2"], ["x2t"], ["rt"], ["top"], ["rank"]]
        banks_of = {"x0t": 1, "lin": 2, "tri": 1, "num": 2, "ct": 1, "wo": 1, "x1t": 1, "q": 1, "sc": 4,
                    "pt": 4, "pv": 1, "at": 1, "wout": 1, "x2t": 1, "rt": 1, "rank": 1}
    order = wavefront(groups)
    plan = BankPlan([(s, b, n) for s, b in order for n in range(banks_of.get(s, 0))], list(range(8)))
    score_scale = 1.0 if first else float(XD) ** -0.5
    E = experts

    with ExitStack() as ctx:
        def sb(name, shape):
            return ctx.enter_context(nc.sbuf_tensor(f"{name}_{layer}", shape, F32))

        def sem(name):
            return take(nc, sems, f"{name}_{layer}")

        psum = [ctx.enter_context(nc.psum_tensor(f"bank{k}_{layer}", [P, 512], F32)) for k in range(8)]

        ident = sb("ident", [P, P])
        head_mask = sb("head_mask", [P, P // XD])
        keys = spare[:, 0:NB * KC * 8 * CTX].rearrange("p (b g n) -> p b g n", b=NB, g=KC)
        vals = sb("vals", [CTX, NB, XH, VW])
        wout = sb("wout", [P, KC, DM])
        bout = sb("bout", [P, DM])
        router = sb("router", [P, KC, E])
        half = sb("half", [P, 1])
        eps = sb("eps", [P, 1])
        spot = sb("spot", [P, 1])
        gspot = sb("gspot", [P, NB, 2])
        unit = sb("unit", [P, 1])
        if first:
            decay = sb("decay", [P, 4, 2, P])
            decay_q = sb("decay_q", [P, 2, P])
            decay_k = sb("decay_k", [P, DM])
            decay_s = sb("decay_s", [P, 2])
            block_mask = sb("block_mask", [P, P])
            wqkv = sb("wqkv", [P, KC, 3 * DM])
            wqk, wkv = wqkv[:, :, 0:2 * DM], wqkv[:, :, DM:3 * DM]
            wo = sb("wo", [P, KC, DM])
            ones = sb("ones", [1, P])
            router_b = sb("router_b", [1, E])
            b2 = sb("b2", [E, DM])
            sb2 = sb("sb2", [P, 2, DM])
            ctx_t = sb("ctx_t", [P, NB, KC, CTX])
            state = sb("state", [P, NB, 2, P])
        else:
            causal = sb("causal", [P, P])
            wqk = sb("wqk", [P, KC, 2 * MEM])
            wkv = sb("wkv", [P, KC, 2 * MEM])
            wo = sb("wo", [MEM, DM])
            wq = sb("wq", [P, KC, DM])
            wk = sb("wk", [P, KC, DM])
            wv = sb("wv", [P, KC, DM])
            ctx_t = sb("ctx_t", [P, NB, KC, CTX])
            key_t = sb("key_t", [P, NB, KC, CTX])
            memory = sb("memory", [MEM, MEM + 1])
            mem_norm = sb("mem_norm", [P, MEM])
            gate = sb("gate", [P, 1])
            mixw = sb("mixw", [P, 2])
            small = sb("small", [P, 4])
            iota = sb("iota", [P, E])
            state = sb("state", [MEM, NB, MEM + 1])

        x = sb("x", [P, NB, DM])
        xt = sb("xt", [P, NB, KC, P])
        x1 = sb("x1", [P, NB, DM])
        x1b = sb("x1b", [P, NB, DM])
        x1t = sb("x1t", [P, NB, KC, P])
        if first:
            qk = sb("qk", [P, NB, 4, P])
            qd = sb("qd", [P, NB, 2, P])
            kd = sb("kd", [P, NB, DM])
            v = sb("v", [P, NB, DM])
            ot = qd
            upd = sb("upd", [P, 2, P])
            cwt = sb("cwt", [E, NB, P])
            xr = sb("xr", [P, NB, DM])
        else:
            neg_t = sb("neg_t", [MEM, NB, 2 * P])
            neg = sb("neg", [P, NB, MEM])
            sig = sb("sig", [MEM, NB, 2, P])
            sigk = sb("sigk", [P, NB, MEM])
            v = sb("v", [P, NB, MEM + 1])
            tri = sb("tri", [P, NB, P])
            den = sb("den", [P, NB, 6])
            comb = sb("comb", [P, NB, MEM])
            combt = sb("combt", [MEM, NB, P])
            qt = sb("qt", [P, NB, KC, P])
            top_i = sb("top_i", [P, NB, 8])
            top_u = ctx.enter_context(nc.sbuf_tensor(f"top_u_{layer}", [P, NB, 8], mybir.dt.uint32))
            hot = sb("hot", [P, NB, K1, E])
            before = sb("before", [P, P])
            ones_sq = sb("ones_sq", [P, P])
            list_at = sb("list_at", [P, E])
            chosen = sb("chosen", [P, NB, E])
            counts = sb("counts", [P, NB + 1, E])
            dest = sb("dest", [P, NB, K1])
            place = sb("place", [P, NB, E])
            placed = sb("placed", [P, NB, K1, E])
            slot = sb("slot", [P, NB, K1])
            slot_u = ctx.enter_context(nc.sbuf_tensor("slot_u", [P, NB, K1], mybir.dt.uint32))
            rows = sb("rows", [P, NB, K1, ROW])
        z = sb("z", [P, NB, DM])
        stats = sb("stats", [P, NB, 6])
        mv = sb("mv", [P, NB, 4])
        peak = sb("peak", [P, 2, XH])
        s = sb("s", [P, 2, XH * CTX])
        pt = sb("pt", [CTX, 2, XH, P])
        if first:
            prob = s[:, :, 0:4 * 2 * P].rearrange("p a (r g n) -> p a r g n", r=4, g=2)
        rsum = sb("rsum", [P, NB, XH])
        att, att_t = z, x1t
        x2 = sb("x2", [P, NB, DM]) if first else rows[:, :, 0, 0:DM]
        x2t = sb("x2t", [P, NB, KC, P])
        nmax = sb("nmax", [P, NB, 1])
        ex = sb("ex", [P, NB, E])
        top8 = sb("top8", [P, NB, 8])
        rest = sb("rest", [P, NB, E])
        tsum = sb("tsum", [P, NB, 2])
        cw = sb("cw", [P, NB, E]) if first else None

        full = [sem(f"full{k}") for k in range(8)]
        free = [sem(f"free{k}") for k in range(8)]
        consts = sem("consts")
        x_in = [sem(f"x_in{b}") for b in range(NB)]
        xt_in = [sem(f"xt_in{b}") for b in range(NB)] if first else None
        sent = [sem(f"sent{b}") for b in range(NB)]
        prep = sem("prep")
        prep_pe = None if first else sem("prep_pe")
        prep_pool = sem("prep_pool")
        gate_exp = None if first else sem("gate_exp")
        vchain = sem("vchain")
        gchain = sem("gchain")
        moved = sem("moved")
        qkd_done = sem("qkd_done") if first else None
        state_done = sem("state_done")
        o_moved = sem("o_moved") if first else None
        mv1_done = sem("mv1_done")
        rstd1 = sem("rstd1")
        x1_done = sem("x1_done")
        x1b_done = sem("x1b_done")
        x1t_done = sem("x1t_done")
        s_done = sem("s_done")
        exp_done = sem("exp_done")
        pta_done = sem("pta_done")
        att_done = sem("att_done")
        att_t_done = sem("att_t_done")
        mv2_done = sem("mv2_done")
        rstd2 = sem("rstd2")
        x2_done = sem("x2_done")
        x2s_done = sem("x2s_done") if first else None
        x2t_done = sem("x2t_done")
        nmax_done = sem("nmax_done")
        ex_done = sem("ex_done")
        cw_done = sem("cw_done") if first else None
        mask_done = None if first else sem("mask_done")
        slot_done = None if first else sem("slot_done")
        copy_done = None if first else sem("copy_done")
        cwt_done = sem("cwt_done") if first else None
        xr_done = sem("xr_done") if first else None
        neg_done = None if first else sem("neg_done")
        nexp_done = None if first else sem("nexp_done")
        combt_done = None if first else sem("combt_done")
        q_done = None if first else sem("q_done")

        def nth(i, b):
            return i * NB + b + 1

        def col(t):
            return t.rearrange("(c p) n -> p c n", p=P)

        loads = [(ident[:], d["ident"]), (head_mask[:], d["head_mask"]), (wout[:], col(d["wout"])),
                 (bout[:], d["bout"]), (router[:], col(d["router"])),
                 (ctx_t[:], d["ctx_t"].rearrange("b (c p) n -> p b c n", p=P))]
        if first:
            loads += [(wqkv[:, :, 0:DM], col(d["wq"])), (wqkv[:, :, DM:2 * DM], col(d["wk"])),
                      (wqkv[:, :, 2 * DM:], col(d["wv"])),
                      (wo[:], col(d["wo"])), (decay[:], d["decay"]), (decay_q[:], d["decay_q"]),
                      (decay_k[:], d["decay_k"]), (decay_s[:], d["decay_s"]), (block_mask[:], d["block_mask"]),
                      (router_b[:], d["router_b"]), (b2[:], d["b2"]), (sb2[:], d["sb2"])]
            loads += [(vals[:, b, :, 0:XD], d["ctx"][b].rearrange("k (h e) -> k h e", e=XD)) for b in range(NB)]
        else:
            loads += [(wqk[:, :, 0:MEM], col(d["wq1"])), (wqk[:, :, MEM:], col(d["wk1"])),
                      (wkv[:, :, 0:MEM], col(d["wk1"])), (wkv[:, :, MEM:], col(d["wv1"])),
                      (wo[:], d["wo1"]), (causal[:], d["causal"]), (wq[:], col(d["wq"])),
                      (wk[:], col(d["wk"])), (wv[:], col(d["wv"])),
                      (memory[:, 0:MEM], d["memory"]), (memory[:, MEM:], d["mem_norm"]),
                      (mem_norm[:], d["mem_norm_rows"]), (gate[:], d["gate"]), (iota[:], d["iota"]),
                      (before[:], d["before"]), (ones_sq[:], d["ones_sq"]), (list_at[:], d["list_at"]),
                      (dest[:], d["dest"])]

        signals = {("qkv", 0): (moved, 1, 1, 0), ("x0t", 0): (moved, 1, 1, 0), ("mix", 0): (o_moved, 1, 1, 0),
                   ("ct", 0): (combt_done, 1, 1, 0), ("x1t", 0): (x1t_done, 1, 1, 0), ("q", 0): (q_done, 1, 1, 0),
                   ("pt", 0): (pta_done, 2, 1, 0), ("pt", 1): (pta_done, 2, 2, 0), ("at", 0): (att_t_done, 1, 1, 0),
                   ("x2t", 0): (x2t_done, 1, 1, 0), ("rt", 0): (ex_done, 1, 1, 0), ("cwt", 0): (cwt_done, 1, 1, 0),
                   ("num", 1): (state_done, 1, 1, NB), ("sc", 3): (s_done, 1, 1, 0), ("pv", 0): (att_done, 1, 1, 0),
                   ("b2", 0): (xr_done, 1, 1, 0)}
        by_place = {place: job for job, place in plan.place.items()}
        unsignalled = {k: [by_place[(k, n)] for n in range(plan.uses[k])
                           if (by_place[(k, n)][0], by_place[(k, n)][2]) not in signals] for k in range(8)}

        def freed(eng, job, i):
            stage, b, n = job
            if (stage, n) in signals:
                signal, per, at, ahead = signals[(stage, n)]
                eng.wait_ge(signal, (i * NB + b) * per + at + ahead)
            else:
                k = plan.bank(job)
                eng.wait_ge(free[k], i * len(unsignalled[k]) + unsignalled[k].index(job) + 1)

        def freed_before(eng, k, i):
            stage, b, n = by_place[(k, plan.uses[k] - 1)]
            if (stage, n) in signals:
                signal, per, at, ahead = signals[(stage, n)]
                eng.wait_ge(signal, i * (NB * per) + ahead)
            else:
                eng.wait_ge(free[k], i * len(unsignalled[k]))

        block = ctx.enter_context(nc.Block())

        @block.sync
        def _(sp):
            def load(b, span):
                sp.dma_start(x[:, b, :], src[b, span, :]).then_inc(x_in[b], 16)
                if first:
                    cols = src_t[b, :, span]
                    sp.dma_start(xt[:, b], cols.rearrange("(c p) n -> p c n", p=P)).then_inc(xt_in[b], 16)

            for dst_ap, src_ap in loads:
                sp.dma_start(dst_ap, src_ap).then_inc(consts, 16)
            for b in range(NB):
                load(b, slice(0, P))
            prefetch(sp)
            with sp.Fori(1, STEPS) as i:
                for b in range(NB):
                    freed(sp, ("wo", b, 0), i - 1)
                    if first:
                        job = ("qkv", b, 1)
                        sp.wait_ge(full[plan.bank(job)], plan.after(job, i - 1))
                    load(b, bass.ds(i * P, P))

        def out_dmas(eng, i, b, what):
            rows = bass.ds(b * SEQ + i * P, P)
            if what == "cols":
                eng.wait_ge(x2t_done, nth(i, b))
                eng.dma_start(dst_t[:, rows].rearrange("(c p) n -> p c n", p=P), x2t[:, b]).then_inc(sent[b], 16)
            if what == "cw":
                eng.wait_ge(cwt_done, nth(i, b))
                carry_pool(eng, gspot[:, b])
                eng.dma_start(dst_cw[:, rows], cwt[:, b]).then_inc(sent[b], 16)
            if what == "rows":
                eng.wait_ge(xr_done if first else x2_done, nth(i, b))
                eng.dma_start(dst[rows, :], (xr if first else x2)[:, b, :]).then_inc(sent[b], 16)

        @block.gpsimd
        def _(pool):
            chain = Chain(pool, gchain, 2 * NB)
            nc.gpsimd.memset(half[:], -0.5)
            nc.gpsimd.memset(gspot[:], 0.0)
            nc.gpsimd.memset(unit[:], 1.0)
            nc.gpsimd.memset(eps[:], LN_EPS).then_inc(prep_pool, 1)
            if first:
                nc.gpsimd.memset(ones[:], 1.0).then_inc(prep_pool, 1)
            pool.wait_ge(prep_pool, 2 if first else 1)
            pool.wait_ge(consts, 16 * len(loads))
            if first:
                nc.gpsimd.tensor_tensor(sb2[:, 0], sb2[:, 0], sb2[:, 1], ALU.add).then_inc(prep_pool, 1)
                pool.wait_ge(prep_pool, 3)
            with pool.Fori(0, STEPS) as i:
                chain.start(i)
                for stage, b in order:
                    if stage in ("wo", "wout"):
                        one = stage == "wo"
                        pool.wait_ge(mv1_done if one else mv2_done, nth(i, b))
                        chain(nc.gpsimd.tensor_tensor(mv[:, b, 2:3], mv[:, b, 1:2], eps[:], ALU.add))
                        nc.gpsimd.tensor_tensor(mv[:, b, 3:4], mv[:, b, 2:3], half[:], ALU.pow)\
                            .then_inc(rstd1 if one else rstd2, 1)
                    if stage == "ln1":
                        pool.wait_ge(x1_done, nth(i, b))
                        nc.gpsimd.tensor_tensor(x1b[:, b], x1[:, b], bout[:], ALU.add).then_inc(x1b_done, 1)
                    if stage == "ln2" and not first:
                        pool.wait_ge(x2_done, nth(i, b))
                        nc.gpsimd.tensor_tensor(rows[:, b, 1, 0:DM], x2[:, b], unit[:].broadcast_to([P, DM]), ALU.mult).then_inc(copy_done, 1)
                    if stage == "ln2" and first:
                        pool.wait_ge(x2_done, nth(i, b))
                        nc.gpsimd.tensor_tensor(x1b[:, b], x2[:, b], sb2[:, 0], ALU.add).then_inc(x2s_done, 1)
                if first:
                    for what in ("cols", "cw", "rows"):
                        for b in range(NB):
                            out_dmas(pool, i, b, what)
                else:
                    for b in range(NB):
                        out_dmas(pool, i, b, "rows")
                        pool.wait_ge(slot_done, nth(i, b))
                        pool.wait_ge(copy_done, nth(i, b))
                        carry_pool(pool, gspot[:, b])
                        for k in range(K1):
                            pool.indirect_dma_start(
                                out=lists, out_offset=bass.IndirectOffsetOnAxis(ap=slot_u[:, b, k:k + 1], axis=0),
                                in_=rows[:, b, k, :], in_offset=None).then_inc(sent[b], 16)
            for b in range(NB):
                pool.wait_ge(sent[b], 48 * STEPS)

        @block.scalar
        def _(act):
            if not first:
                act.wait_ge(consts, 16 * len(loads))
                nc.scalar.activation(small[:, 0:1], gate[:], ACT.Exp, scale=-1.0).then_inc(gate_exp, 1)
            with act.Fori(0, STEPS) as i:
                for stage, b in order:
                    def bank(n=0, stage=stage, b=b):
                        job = (stage, b, n)
                        act.wait_ge(full[plan.bank(job)], plan.after(job, i))
                        return psum[plan.bank(job)]

                    def move(out, in_, done):
                        nc.scalar.activation(out, in_, ACT.Copy).then_inc(done, 1)

                    if stage == "qkv":
                        move(qk[:, b], bank(0)[:].rearrange("p (a n) -> p a n", a=4), moved)
                    if stage == "x0t":
                        move(xt[:, b], bank()[:, 0:DM].rearrange("p (c n) -> p c n", c=KC), moved)
                    if stage == "mix":
                        move(ot[:, b], bank(0)[:, 0:2 * P].rearrange("p (g n) -> p g n", g=2), o_moved)
                    if stage == "lin":
                        act.wait_ge(neg_done, nth(i, b))
                        nc.scalar.activation(neg_t[:, b], neg_t[:, b], ACT.Exp)
                        nc.scalar.activation(neg[:, b], neg[:, b], ACT.Exp)\
                            .then_inc(nexp_done, 1)
                    if stage == "ct":
                        move(combt[:, b], bank()[0:MEM, 0:P], combt_done)
                    if stage == "x1t":
                        move(x1t[:, b], bank()[:, 0:DM].rearrange("p (c n) -> p c n", c=KC), x1t_done)
                    if stage == "q":
                        move(qt[:, b], bank()[:, 0:DM].rearrange("p (c n) -> p c n", c=KC), q_done)
                    if stage == "sc":
                        act.wait_ge(s_done, nth(i, b))
                        nc.scalar.activation(s[:, b % 2], s[:, b % 2], ACT.Exp, scale=score_scale)\
                            .then_inc(exp_done, 1)
                    if stage == "pt":
                        for n in (0, 1):
                            move(pt[:, b % 2, 4 * n:4 * n + 4], bank(n)[0:CTX, :].rearrange("p (h n) -> p h n", h=4),
                                 pta_done)
                    if stage == "at":
                        move(att_t[:, b], bank()[:, 0:DM].rearrange("p (c n) -> p c n", c=KC), att_t_done)
                    if stage == "x2t":
                        if first:
                            act.wait_ge(sent[b], i * 48)
                        move(x2t[:, b], bank()[:, 0:DM].rearrange("p (c n) -> p c n", c=KC), x2t_done)
                    if stage == "rt":
                        act.wait_ge(nmax_done, nth(i, b))
                        nc.scalar.activation(ex[:, b], bank()[:, 0:E], ACT.Exp, bias=nmax[:, b])\
                            .then_inc(ex_done, 1)
                    if stage == "cwt":
                        act.wait_ge(sent[b], i * 48)
                        move(cwt[:, b], bank()[0:E, 0:P], cwt_done)

        @block.vector
        def _(dve):
            chain = Chain(dve, vchain, VCHAIN[layer])
            plain = [0]

            def done(ins):
                plain[0] += 1
                ins.then_inc(prep, 1)
                dve.wait_ge(prep, plain[0])

            for b in range(NB):
                nc.vector.memset(state[:, b], 0.0).then_inc(state_done, 1)
            if not first:
                done(nc.vector.memset(rows[:], 0.0))
                done(nc.vector.memset(counts[:], 0.0))
                done(nc.vector.memset(v[:], 1.0))
                done(nc.vector.memset(vals[:], 1.0))
            dve.wait_ge(consts, 16 * len(loads))
            if first:
                for b in range(NB):
                    done(nc.vector.memset(vals[:, b, :, XD:], 1.0))
            else:
                dve.wait_ge(gate_exp, 1)
                done(nc.vector.tensor_scalar(small[:, 1:2], small[:, 0:1], 1.0, None, ALU.add))
                done(nc.vector.reciprocal(small[:, 2:3], small[:, 1:2]))
                done(nc.vector.tensor_scalar(mixw[:, 0:1], small[:, 2:3], -1.0, 1.0, ALU.mult, ALU.add))
                done(nc.vector.tensor_reduce(small[:, 3:4], mem_norm[:], AX.X, ALU.add))
                done(nc.vector.tensor_scalar(small[:, 3:4], small[:, 3:4], CLIP, None, ALU.is_ge))
                done(nc.vector.tensor_tensor(mixw[:, 1:2], small[:, 3:4], small[:, 2:3], ALU.mult))
                for b in range(NB):
                    dve.wait_ge(prep_pe, 1 + 2 * b)
                    done(nc.vector.tensor_copy(key_t[:, b], psum[2 * b][:, 0:KC * CTX]
                                               .rearrange("p (c n) -> p c n", c=KC)))
                    dve.wait_ge(prep_pe, 2 + 2 * b)
                    done(nc.vector.tensor_copy(vals[:, b, :, 0:XD], psum[2 * b + 1][0:CTX, 0:DM]
                                               .rearrange("p (h e) -> p h e", e=XD)))
            for b in range(NB):
                for g in range(KC):
                    kin = (ctx_t if first else key_t)[:, b, g].unsqueeze(1).broadcast_to([P, 8, CTX])
                    mask = head_mask[:].unsqueeze(2).broadcast_to([P, 8, CTX])
                    done(nc.vector.tensor_tensor(keys[:, b, g].rearrange("p (h k) -> p h k", h=8),
                                                 kin, mask, ALU.mult))
            assert plain[0] == VPREP[layer], plain[0]

            with dve.Fori(0, STEPS) as i:
                chain.start(i)
                for stage, b in order:
                    def bank(n=0, stage=stage, b=b):
                        job = (stage, b, n)
                        dve.wait_ge(full[plan.bank(job)], plan.after(job, i))
                        return psum[plan.bank(job)]

                    def frees(ins, n=0, stage=stage, b=b):
                        ins.then_inc(free[plan.bank((stage, b, n))], 1)

                    def norm_sums(rows, done_sem):
                        frees(nc.vector.tensor_tensor(z[:, b], bank()[:, 0:DM], rows, ALU.add))
                        freed(dve, (stage, b, 0), i)
                        chain(nc.vector.bn_stats(stats[:, b], z[:, b]), carrier=spot[:])
                        nc.vector.bn_aggr(mv[:, b, 0:2], stats[:, b]).then_inc(done_sem, 1)

                    def norm(out, rstd, done_sem):
                        dve.wait_ge(rstd, nth(i, b))
                        nc.vector.tensor_scalar(out, z[:, b], mv[:, b, 0:1], mv[:, b, 3:4],
                                                ALU.subtract, ALU.mult).then_inc(done_sem, 1)

                    if stage == "qkv":
                        kv = bank(1)
                        nc.vector.tensor_tensor(kd[:, b], kv[:, 0:DM], decay_k[:], ALU.mult)
                        frees(nc.vector.tensor_copy(v[:, b], kv[:, DM:2 * DM]), 1)
                        dve.wait_ge(moved, nth(i, b))
                        nc.vector.tensor_tensor(qd[:, b], qk[:, b, 0:2], decay_q[:], ALU.mult).then_inc(qkd_done, 1)
                    if stage == "ret":
                        for n in range(4):
                            frees(nc.vector.tensor_tensor(prob[:, b % 2, n],
                                                          bank(n)[:, 0:2 * P].rearrange("p (g n) -> p g n", g=2),
                                                          decay[:, n], ALU.mult), n)
                    if stage == "mix":
                        dve.wait_ge(state_done, nth(i, b) + NB - 1)
                        frees(nc.vector.tensor_tensor(upd[:], bank(1)[:, 0:2 * P].rearrange("p (g n) -> p g n", g=2),
                                                      block_mask[:].unsqueeze(1).broadcast_to([P, 2, P]),
                                                      ALU.mult), 1)
                        freed(dve, ("mix", b, 1), i)
                        for g in range(2):
                            ins = nc.vector.scalar_tensor_tensor(out=state[:, b, g], in0=state[:, b, g],
                                                                 scalar=decay_s[:, g:g + 1], in1=upd[:, g],
                                                                 op0=ALU.mult, op1=ALU.add)
                        ins.then_inc(state_done, 1)
                    if stage == "lin":
                        qk_ps, kv_ps = bank(0), bank(1)
                        nc.vector.tensor_scalar(neg_t[:, b], qk_ps[0:MEM, 0:2 * P], 0.0, None, ALU.min)
                        nc.vector.tensor_scalar(neg[:, b], kv_ps[:, 0:MEM], 0.0, None, ALU.min)\
                            .then_inc(neg_done, 1)
                        nc.vector.tensor_copy(v[:, b, 0:MEM], kv_ps[:, MEM:2 * MEM])
                        dve.wait_ge(nexp_done, nth(i, b))
                        frees(nc.vector.scalar_tensor_tensor(
                            out=sig[:, b], in0=qk_ps[0:MEM, 0:2 * P].rearrange("p (a n) -> p a n", a=2), scalar=0.0,
                            in1=neg_t[:, b].rearrange("p (a n) -> p a n", a=2),
                            op0=ALU.max, op1=ALU.add), 0)
                        frees(nc.vector.scalar_tensor_tensor(
                            out=sigk[:, b], in0=kv_ps[:, 0:MEM], scalar=0.0, in1=neg[:, b],
                            op0=ALU.max, op1=ALU.add), 1)
                    if stage == "tri":
                        frees(nc.vector.tensor_tensor(tri[:, b], bank()[:, 0:P], causal[:], ALU.mult))
                    if stage == "num":
                        nu = bank(0)
                        two = nu[:, 0:2 * (MEM + 1)].rearrange("p (a n) -> p a n", a=2)
                        chain(nc.vector.tensor_scalar(den[:, b, 0:2], two[:, :, MEM], CLIP, None, ALU.max))
                        chain(nc.vector.reciprocal(den[:, b, 2:4], den[:, b, 0:2]))
                        chain(nc.vector.tensor_tensor(den[:, b, 4:6], den[:, b, 2:4], mixw[:], ALU.mult))
                        chain(nc.vector.tensor_scalar(comb[:, b], two[:, 0, 0:MEM], den[:, b, 4:5], None, ALU.mult))
                        frees(nc.vector.scalar_tensor_tensor(out=comb[:, b], in0=two[:, 1, 0:MEM],
                                                             scalar=den[:, b, 5:6], in1=comb[:, b],
                                                             op0=ALU.mult, op1=ALU.add), 0)
                        nc.vector.tensor_tensor(state[:, b], state[:, b], bank(1)[0:MEM, 0:MEM + 1], ALU.add)\
                            .then_inc(state_done, 1)
                    if stage == "wo":
                        dve.wait_ge(x_in[b], i * 16 + 16)
                        norm_sums(x[:, b], mv1_done)
                    if stage == "ln1":
                        norm(x1[:, b], rstd1, x1_done)
                    if stage == "sc":
                        for n in range(4):
                            ins = nc.vector.tensor_reduce(peak[:, b % 2, 4 * n:4 * n + 4],
                                                          bank(n)[:, 0:QH].rearrange("p (h k) -> p h k", h=4),
                                                          AX.X, ALU.max)
                        chain(ins)
                        for n in range(4):
                            ins = nc.vector.tensor_tensor(
                                s[:, b % 2, n * QH:(n + 1) * QH].rearrange("p (h k) -> p h k", h=4),
                                bank(n)[:, 0:QH].rearrange("p (h k) -> p h k", h=4),
                                peak[:, b % 2, 4 * n:4 * n + 4].unsqueeze(2).broadcast_to([P, 4, CTX]), ALU.subtract)
                            if n < 3:
                                frees(ins, n)
                        ins.then_inc(s_done, 1)
                    if stage == "pt":
                        for n in (2, 3):
                            frees(nc.vector.tensor_copy(pt[:, b % 2, 4 * n:4 * n + 4],
                                                        bank(n)[0:CTX, :].rearrange("p (h n) -> p h n", h=4)), n)
                    if stage == "pv":
                        o = bank()[:, 0:XH * VW].rearrange("p (h e) -> p h e", e=VW)
                        chain(nc.vector.reciprocal(rsum[:, b], o[:, :, XD]))
                        nc.vector.tensor_tensor(att[:, b].rearrange("p (h e) -> p h e", e=XD), o[:, :, 0:XD],
                                                rsum[:, b].unsqueeze(2).broadcast_to([P, XH, XD]), ALU.mult)\
                            .then_inc(att_done, 1)
                    if stage == "wout":
                        dve.wait_ge(x1b_done, nth(i, b))
                        norm_sums(x1b[:, b], mv2_done)
                    if stage == "ln2":
                        if not first:
                            dve.wait_ge(sent[b], i * 48)
                        norm(x2[:, b], rstd2, x2_done)
                    if stage == "rt":
                        nc.vector.tensor_reduce(nmax[:, b], bank()[:, 0:E], AX.X, ALU.max, negate=True)\
                            .then_inc(nmax_done, 1)
                    if stage == "top":
                        dve.wait_ge(ex_done, nth(i, b))
                        carry(dve, spot[:])
                        chain(nc.vector.max(top8[:, b], ex[:, b]))
                        chain(nc.vector.tensor_reduce(tsum[:, b, 0:1], top8[:, b, 0:top], AX.X, ALU.add))
                        chain(nc.vector.reciprocal(tsum[:, b, 1:2], tsum[:, b, 0:1]))
                        if first:
                            dve.wait_ge(cwt_done, i * NB)
                            carry(dve, spot[:])
                            chain(nc.vector.match_replace(rest[:, b], top8[:, b], ex[:, b], -1.0))
                            chain(nc.vector.tensor_scalar(rest[:, b], rest[:, b], 0.0, tsum[:, b, 1:2],
                                                          ALU.is_lt, ALU.mult))
                        else:
                            carry(dve, spot[:])
                            chain(nc.vector.max_index(top_u[:, b], top8[:, b], ex[:, b]))
                            chain(nc.vector.tensor_copy(top_i[:, b], top_u[:, b]))
                            for k in range(K1):
                                chain(nc.vector.tensor_scalar(hot[:, b, k], iota[:], top_i[:, b, k:k + 1],
                                                              None, ALU.is_equal))
                            nc.vector.tensor_scalar(rows[:, b, :, DM + 1], top8[:, b, 0:K1], tsum[:, b, 1:2], None,
                                                    ALU.mult)
                            chain(nc.vector.tensor_copy(rows[:, b, :, DM], dest[:, b]))
                            nc.vector.tensor_scalar(dest[:, b], dest[:, b], float(P), None, ALU.add)
                            chain(nc.vector.tensor_tensor(chosen[:, b], hot[:, b, 0], hot[:, b, 1], ALU.add))
                            nc.vector.tensor_tensor(counts[:, b + 1], counts[:, b], chosen[:, b], ALU.add)\
                                .then_inc(mask_done, 1)
                            dve.wait_ge(mask_done, nth(i, b))
                        if first:
                            nc.vector.tensor_tensor(cw[:, b], rest[:, b], ex[:, b], ALU.mult).then_inc(cw_done, 1)
                    if stage == "rank":
                        frees(nc.vector.tensor_tensor(place[:, b], bank()[:, 0:E], list_at[:], ALU.add))
                        freed(dve, ("rank", b, 0), i)
                        chain(nc.vector.tensor_tensor(placed[:, b], hot[:, b],
                                                      place[:, b].unsqueeze(1).broadcast_to([P, K1, E]), ALU.mult))
                        chain(nc.vector.tensor_reduce(slot[:, b], placed[:, b], AX.X, ALU.add))
                        nc.vector.tensor_copy(slot_u[:, b], slot[:, b]).then_inc(slot_done, 1)
                        if b == NB - 1:
                            nc.vector.tensor_copy(counts[:, 0], counts[:, NB]).then_inc(prep, 1)
                            dve.wait_ge(prep, VPREP[layer] + 1 + i)
                    if stage == "b2":
                        dve.wait_ge(x2s_done, nth(i, b))
                        dve.wait_ge(sent[b], i * 48)
                        nc.vector.tensor_tensor(xr[:, b], bank()[:, 0:DM], x1b[:, b], ALU.add).then_inc(xr_done, 1)

            if not first:
                nc.vector.tensor_copy(listed, counts[:, 0])

        @block.tensor
        def _(pe):
            mm, tr = nc.tensor.matmul, nc.tensor.transpose
            pe.wait_ge(consts, 16 * len(loads))
            if not first:
                for b in range(NB):
                    for g in range(KC):
                        for c in range(KC):
                            ins = mm(psum[2 * b][:, g * CTX:(g + 1) * CTX], wk[:, c, g * P:(g + 1) * P],
                                     ctx_t[:, b, c], start=c == 0, stop=c == KC - 1)
                    ins.then_inc(prep_pe, 1)
                    for c in range(KC):
                        ins = mm(psum[2 * b + 1][0:CTX, 0:DM], ctx_t[:, b, c], wv[:, c],
                                 start=c == 0, stop=c == KC - 1)
                    ins.then_inc(prep_pe, 1)
            else:
                pe.wait_ge(prep_pool, 3)
            pe.wait_ge(prep, VPREP[layer])
            with pe.Fori(0, STEPS) as i:
                for stage, b in order:
                    def bank(n=0, stage=stage, b=b):
                        k, use = plan.place[(stage, b, n)]
                        if use:
                            freed(pe, by_place[(k, use - 1)], i)
                        else:
                            freed_before(pe, k, i)
                        return psum[k]

                    def fills(ins, n=0, stage=stage, b=b):
                        ins.then_inc(full[plan.bank((stage, b, n))], 1)

                    if stage == "qkv":
                        pe.wait_ge(xt_in[b], i * 16 + 16)
                        out = bank(0)
                        for a in range(4):
                            for c in range(KC):
                                ins = mm(out[:, a * P:(a + 1) * P], wqk[:, c, a * P:(a + 1) * P], xt[:, b, c],
                                         start=c == 0, stop=c == KC - 1)
                        fills(ins, 0)
                        out = bank(1)
                        for c in range(KC):
                            ins = mm(out[:], xt[:, b, c], wkv[:, c], start=c == 0, stop=c == KC - 1)
                        fills(ins, 1)
                    if stage == "ret":
                        pe.wait_ge(moved, nth(i, b))
                        outs = [bank(r) for r in range(4)]
                        for g in range(2):
                            for r in range(4):
                                rows = slice(RD * r, RD * (r + 1))
                                ins = mm(outs[r][:, g * P:(g + 1) * P], qk[rows, b, 2 + g], qk[rows, b, g],
                                         start=True, stop=True)
                                if g == 1:
                                    fills(ins, r)
                    if stage == "mix":
                        pe.wait_ge(qkd_done, nth(i, b))
                        pe.wait_ge(state_done, nth(i, b))
                        out = bank(0)
                        for g in range(2):
                            mm(out[:, g * P:(g + 1) * P], state[:, b, g], qd[:, b, g], start=g == 0, stop=False,
                               skip_group_check=True)
                        for n in range(4):
                            freed(pe, ("ret", b, n), i)
                        for g in range(2):
                            for r in range(4):
                                h = 4 * g + r
                                ins = mm(out[RD * r:RD * (r + 1), g * P:(g + 1) * P], v[:, b, h * RD:(h + 1) * RD],
                                         prob[:, b % 2, r, g], start=False, stop=True, skip_group_check=True)
                        fills(ins, 0)
                        out = bank(1)
                        for g in range(2):
                            ins = mm(out[:, g * P:(g + 1) * P], kd[:, b, g * P:(g + 1) * P],
                                     v[:, b, g * P:(g + 1) * P], start=True, stop=True)
                        fills(ins, 1)
                    if stage == "x0t":
                        pe.wait_ge(x_in[b], i * 16 + 16)
                        out = bank()
                        for c in range(KC):
                            ins = tr(out[:, c * P:(c + 1) * P], x[:, b, c * P:(c + 1) * P], ident[:])
                        fills(ins)
                    if stage == "lin":
                        pe.wait_ge(moved, nth(i, b))
                        out = bank(0)
                        for a in range(2):
                            for c in range(KC):
                                ins = mm(out[0:MEM, a * P:(a + 1) * P], wqk[:, c, a * MEM:(a + 1) * MEM], xt[:, b, c],
                                         start=c == 0, stop=c == KC - 1)
                        fills(ins, 0)
                        out = bank(1)
                        for c in range(KC):
                            ins = mm(out[:, 0:2 * MEM], xt[:, b, c], wkv[:, c], start=c == 0, stop=c == KC - 1)
                        fills(ins, 1)
                    if stage == "tri":
                        freed(pe, ("lin", b, 0), i)
                        fills(mm(bank()[:, 0:P], sig[:, b, 1], sig[:, b, 0], start=True, stop=True))
                    if stage == "num":
                        freed(pe, ("tri", b, 0), i)
                        freed(pe, ("lin", b, 1), i)
                        pe.wait_ge(state_done, nth(i, b))
                        out = bank(0)
                        mm(out[:, MEM + 1:2 * (MEM + 1)], sig[:, b, 0], memory[:], start=True, stop=True)
                        mm(out[:, 0:MEM + 1], sig[:, b, 0], state[:, b], start=True, stop=False)
                        fills(mm(out[:, 0:MEM + 1], tri[:, b], v[:, b], start=False, stop=True), 0)
                        fills(mm(bank(1)[0:MEM, 0:MEM + 1], sigk[:, b], v[:, b], start=True, stop=True), 1)
                    if stage == "ct":
                        freed(pe, ("num", b, 0), i)
                        out = bank()
                        fills(mm(out[0:MEM, 0:P], comb[:, b], ident[:], start=True, stop=True))
                    if stage == "wo":
                        out = bank()
                        if first:
                            pe.wait_ge(o_moved, nth(i, b))
                            for c in range(KC):
                                ins = mm(out[:, 0:DM], ot[:, b, c], wo[:, c], start=c == 0, stop=c == KC - 1)
                        else:
                            pe.wait_ge(combt_done, nth(i, b))
                            ins = mm(out[:, 0:DM], combt[:, b], wo[:], start=True, stop=True)
                        fills(ins)
                    if stage in ("x1t", "at", "x2t"):
                        ready, rows = {"x1t": (x1_done, x1), "at": (att_done, att), "x2t": (x2_done, x2)}[stage]
                        pe.wait_ge(ready, nth(i, b))
                        out = bank()
                        for c in range(KC):
                            ins = tr(out[:, c * P:(c + 1) * P], rows[:, b, c * P:(c + 1) * P], ident[:])
                        fills(ins)
                    if stage == "q":
                        pe.wait_ge(x1t_done, nth(i, b))
                        out = bank()
                        for g in range(KC):
                            for c in range(KC):
                                ins = mm(out[:, g * P:(g + 1) * P], wq[:, c, g * P:(g + 1) * P], x1t[:, b, c],
                                         start=c == 0, stop=c == KC - 1)
                        fills(ins)
                    if stage == "sc":
                        pe.wait_ge(x1t_done if first else q_done, nth(i, b))
                        for n in range(4):
                            g = n // 2
                            fills(mm(bank(n)[:, 0:QH], (x1t if first else qt)[:, b, g],
                                     keys[:, b, g, (n % 2) * QH:(n % 2 + 1) * QH], start=True, stop=True), n)
                    if stage == "pt":
                        pe.wait_ge(exp_done, nth(i, b))
                        for n in range(4):
                            out = bank(n)
                            for j in range(4):
                                h = 4 * n + j
                                ins = tr(out[0:CTX, j * P:(j + 1) * P], s[:, b % 2, h * CTX:(h + 1) * CTX], ident[:])
                            fills(ins, n)
                    if stage == "pv":
                        pe.wait_ge(pta_done, 2 * nth(i, b))
                        freed(pe, ("pt", b, 2), i)
                        freed(pe, ("pt", b, 3), i)
                        out = bank()
                        for h in range(XH):
                            ins = mm(out[:, h * VW:(h + 1) * VW], pt[:, b % 2, h], vals[:, b, h],
                                     start=True, stop=True)
                        fills(ins)
                    if stage == "wout":
                        pe.wait_ge(att_t_done, nth(i, b))
                        out = bank()
                        for c in range(KC):
                            ins = mm(out[:, 0:DM], att_t[:, b, c], wout[:, c], start=c == 0, stop=c == KC - 1)
                        fills(ins)
                    if stage == "rt":
                        pe.wait_ge(x2t_done, nth(i, b))
                        out = bank()
                        for c in range(KC):
                            ins = mm(out[:, 0:E], x2t[:, b, c], router[:, c], start=c == 0,
                                     stop=c == KC - 1 and not first)
                        if first:
                            ins = mm(out[:, 0:E], ones[:], router_b[:], start=False, stop=True)
                        fills(ins)
                    if stage == "rank":
                        pe.wait_ge(mask_done, nth(i, b))
                        out = bank()
                        mm(out[:, 0:E], before[:], chosen[:, b], start=True, stop=False)
                        fills(mm(out[:, 0:E], ones_sq[:], counts[:, b], start=False, stop=True))
                    if stage == "cwt":
                        pe.wait_ge(cw_done, nth(i, b))
                        out = bank()
                        fills(mm(out[0:E, 0:P], cw[:, b], ident[:], start=True, stop=True))
                    if stage == "b2":
                        pe.wait_ge(cwt_done, nth(i, b))
                        fills(mm(bank()[:, 0:DM], cwt[:, b], b2[:], start=True, stop=True))


TOK = 512
SUB = TOK // P
TILES = NT // TOK


def shared_routed_phase(nc, sems, d, w1, w2, w_in, src, src_t, src_cw, dst):
    PAIRS, CH = E0 // 2, ES * HS // P
    UNITS = CH + PAIRS
    G = 4
    GROUPS = PAIRS // G
    with ExitStack() as ctx:
        def sb(name, shape):
            return ctx.enter_context(nc.sbuf_tensor(f"b_{name}", shape, F32))

        def sem(name):
            return take(nc, sems, f"b_{name}")

        hp = [ctx.enter_context(nc.psum_tensor(f"b_hp{k}", [P, 512], F32)) for k in range(4)]
        yp = [ctx.enter_context(nc.psum_tensor(f"b_yp{k}", [P, 512], F32)) for k in range(4)]
        sw1 = sb("sw1", [P, KC, ES * HS])
        sw2 = sb("sw2", [P, CH, DM])
        b1 = sb("b1", [P, PAIRS])
        sb1 = sb("sb1", [P, CH])
        half = sb("half", [P, 1])
        eps = sb("eps", [P, 1])
        spot = sb("spot", [P, 1])
        xt = sb("xt", [P, 2, KC, TOK])
        xr = sb("xr", [P, 2, SUB, DM])
        cw = sb("cw", [P, 2, G, TOK])
        h = sb("h", [P, 4, TOK])
        acc = sb("acc", [P, SUB, DM])
        stats = sb("stats", [P, SUB, 6])
        mv = sb("mv", [P, SUB, 4])
        out = sb("out", [P, SUB, DM])

        consts = sem("consts")
        xt_in = [sem(f"xt_in{k}") for k in range(2)]
        row_in = [sem(f"row_in{k}") for k in range(2)]
        cw_in = [sem(f"cw_in{k}") for k in range(2)]
        h_full = sem("h_full")
        h_done = sem("h_done")
        hw_done = sem("hw_done")
        h_used = sem("h_used")
        y_full = sem("y_full")
        y_used = sem("y_used")
        st_done = sem("st_done")
        mv_done = sem("mv_done")
        ve_done = sem("ve_done")
        rstd = sem("rstd")
        out_done = sem("out_done")
        sent = sem("sent")
        half_done = sem("half_done")

        loads = [(sw1[:, :, e * HS:(e + 1) * HS], d["sw1"][e].rearrange("(c p) n -> p c n", p=P)) for e in range(ES)]
        loads += [(sw2[:], d["sw2"].rearrange("e (c p) n -> p (e c) n", p=P)), (b1[:], d["b1"]), (sb1[:], d["sb1"])]
        block = ctx.enter_context(nc.Block())

        @block.sync
        def _(sp):
            def load(k, span):
                sp.dma_start(xt[:, k], src_t[:, span].rearrange("(c p) n -> p c n", p=P)).then_inc(xt_in[k], 16)
                sp.dma_start(xr[:, k], src[span, :].rearrange("(t p) n -> p t n", p=P)).then_inc(row_in[k], 16)

            def load_weights(span, g):
                for e in range(2):
                    rows = src_cw[2 * G * g + e:2 * G * (g + 1):2, span]
                    sp.dma_start(cw[H0 * e:H0 * (e + 1), g % 2], rows.unsqueeze(0).broadcast_to([H0, G, TOK]))\
                        .then_inc(cw_in[g % 2], 16)

            def weights(T, span, gs, first=False):
                for g in gs:
                    if not first:
                        sp.wait_ge(hw_done, T * PAIRS + (g - 1) * G)
                    elif g >= 2:
                        sp.wait_ge(hw_done, (g - 1) * G)
                    load_weights(span, g)

            def tile(T, k):
                span = bass.ds(T * TOK, TOK)
                weights(T, span, range(GROUPS // 2))
                sp.wait_ge(h_full, T * UNITS)
                sp.wait_ge(y_used, T)
                load(k, bass.ds((T + 1) * TOK, TOK))
                weights(T, span, range(GROUPS // 2, GROUPS))

            load(0, slice(0, TOK))
            for a, b in loads:
                sp.dma_start(a, b).then_inc(consts, 16)
            weights(0, slice(0, TOK), range(2), first=True)
            load(1, slice(TOK, 2 * TOK))
            weights(0, slice(0, TOK), range(2, GROUPS), first=True)
            with sp.Fori(0, TILES // 2 - 1) as i:
                for k in range(2):
                    tile(2 * i + k + 1, k)
            weights(TILES - 1, slice((TILES - 1) * TOK, TILES * TOK), range(GROUPS))

        @block.gpsimd
        def _(pool):
            nc.gpsimd.memset(half[:], -0.5)
            nc.gpsimd.memset(eps[:], LN_EPS).then_inc(half_done, 1)
            pool.wait_ge(half_done, 1)
            with pool.Fori(0, TILES) as T:
                pool.wait_ge(mv_done, T + 1)
                nc.gpsimd.tensor_tensor(mv[:, :, 2], mv[:, :, 1], eps[:].broadcast_to([P, SUB]), ALU.add).then_inc(ve_done, 1)
                pool.wait_ge(ve_done, T + 1)
                nc.gpsimd.tensor_tensor(mv[:, :, 3], mv[:, :, 2], half[:].broadcast_to([P, SUB]), ALU.pow)\
                    .then_inc(rstd, 1)
                pool.wait_ge(out_done, T + 1)
                pool.dma_start(dst[bass.ds(T * TOK, TOK), :].rearrange("(t p) n -> p t n", p=P), out[:])\
                    .then_inc(sent, 16)
            pool.wait_ge(sent, 16 * TILES)

        @block.scalar
        def _(act):
            act.wait_ge(consts, 16 * len(loads))
            with act.Fori(0, TILES) as T:
                for u in range(UNITS):
                    act.wait_ge(h_full, T * UNITS + u + 1)
                    if u < 4:
                        act.wait_ge(y_full, T)
                    else:
                        act.wait_ge(h_used, T * (UNITS - 1) + u - 3)
                    bias = sb1[:, u:u + 1] if u < CH else b1[:, u - CH:u - CH + 1]
                    nc.scalar.activation(h[:, u % 4], hp[u % 4][:], ACT.Silu, bias=bias).then_inc(h_done, 1)

        @block.vector
        def _(dve):
            def weigh(T):
                for p in range(PAIRS):
                    g, u = p // G, CH + p
                    if p % G == 0:
                        dve.wait_ge(cw_in[g % 2], 32 * (T * (GROUPS // 2) + g // 2 + 1))
                    dve.wait_ge(h_done, T * UNITS + u + 1)
                    nc.vector.tensor_tensor(h[:, u % 4], h[:, u % 4], cw[:, g % 2, p % G], ALU.mult)\
                        .then_inc(hw_done, 1)

            with dve.Fori(0, TILES // 2) as i:
                for k in range(2):
                    T = 2 * i + k
                    weigh(T)
                    dve.wait_ge(row_in[k], 16 * i + 16)
                    dve.wait_ge(y_full, T + 1)
                    dve.wait_ge(out_done, T)
                    for t in range(SUB):
                        ins = nc.vector.tensor_tensor(acc[:, t], yp[t][:, 0:DM], xr[:, k, t], ALU.add)
                    ins.then_inc(y_used, 1)
                    dve.wait_ge(y_used, T + 1)
                    for t in range(SUB):
                        ins = nc.vector.bn_stats(stats[:, t], acc[:, t])
                    ins.then_inc(st_done, 1)
                    dve.wait_ge(st_done, T + 1)
                    carry(dve, spot[:])
                    for t in range(SUB):
                        ins = nc.vector.bn_aggr(mv[:, t, 0:2], stats[:, t])
                    ins.then_inc(mv_done, 1)
                    dve.wait_ge(rstd, T + 1)
                    dve.wait_ge(sent, T * 16)
                    for t in range(SUB):
                        ins = nc.vector.tensor_scalar(out[:, t], acc[:, t], mv[:, t, 0:1], mv[:, t, 3:4],
                                                      ALU.subtract, ALU.mult)
                    ins.then_inc(out_done, 1)

        @block.tensor
        def _(pe):
            mm = nc.tensor.matmul
            pe.wait_ge(consts, 16 * len(loads))
            pe.wait_ge(w_in, 32)

            def hidden(T, k, u):
                pe.wait_ge(h_done, T * UNITS + max(0, u - 3))
                for c in range(KC):
                    w = sw1[:, c, u * P:(u + 1) * P] if u < CH else w1[:, c, (u - CH) * P:(u - CH + 1) * P]
                    ins = mm(hp[u % 4][:], w, xt[:, k, c], start=c == 0, stop=c == KC - 1)
                ins.then_inc(h_full, 1)

            def outward(T, u):
                if u < CH:
                    pe.wait_ge(h_done, T * UNITS + u + 1)
                else:
                    pe.wait_ge(hw_done, T * PAIRS + u - CH + 1)
                if u == 0:
                    pe.wait_ge(y_used, T)
                for t in range(SUB):
                    ins = mm(yp[t][:, 0:DM], h[:, u % 4, t * P:(t + 1) * P], sw2[:, u] if u < CH else w2[:, u - CH],
                             start=u == 0, stop=u == UNITS - 1)
                ins.then_inc(h_used if u < UNITS - 1 else y_full, 1)

            LAG = 2
            with pe.Fori(0, TILES // 2) as i:
                for k in range(2):
                    T = 2 * i + k
                    pe.wait_ge(xt_in[k], 16 * i + 16)
                    for u in range(UNITS + LAG):
                        if u < UNITS:
                            hidden(T, k, u)
                        if u >= LAG:
                            outward(T, u - LAG)


def gated_phase(nc, sems, d, wg, wu, w_in, lists, listed, results):
    HC = H1 // P
    I32, U32 = mybir.dt.int32, mybir.dt.uint32
    LOOP = (ROWS1 - 2) // 2
    with ExitStack() as ctx:
        def sb(name, shape, dt=F32):
            return ctx.enter_context(nc.sbuf_tensor(f"d_{name}", shape, dt))

        def sem(name):
            return take(nc, sems, f"d_{name}")

        def bank(name):
            return ctx.enter_context(nc.psum_tensor(f"d_{name}", [P, 512], F32))

        gp, up = [bank(f"gp{k}") for k in range(2)], [bank(f"up{k}") for k in range(2)]
        xp, hp, yp, tp = bank("xp"), bank("hp"), bank("yp"), bank("tp")
        wd = sb("wd", [P, E1 * HC, DM])
        ident = sb("ident", [P, P])
        ones_sq = sb("ones_sq", [P, P])
        list_at = sb("list_at", [P, E1])
        tile_no = sb("tile_no", [P, ROWS1])
        padding = sb("padding", [P, 2 * E1, ROW])
        tiles_of = sb("tiles_of", [P, E1])
        ones_row = sb("ones_row", [P, E1])
        ends = sb("ends", [P, E1])
        count_i = sb("count_i", [P, E1], I32)
        tiles_i = sb("tiles_i", [P, E1], I32)
        fill_i = sb("fill_i", [P, E1], I32)
        passed = sb("passed", [P, 2, ROWS1, E1])
        of_tile = sb("of_tile", [P, 5, ROWS1])
        row_i = sb("row_i", [P, ROWS1], I32)
        expert_i = sb("expert_i", [P, ROWS1], I32)
        x = sb("x", [P, 2, ROW])
        xt = sb("xt", [P, 2, KC, P])
        gate = sb("gate", [P, 2, H1])
        h = sb("h", [P, 2, H1])
        ht = sb("ht", [P, 2, HC, P])
        y = sb("y", [P, 2, DM])
        dest = sb("dest", [P, 2], U32)
        weight = sb("weight", [P, 2])

        gspot = sb("gspot", [P, 2, 2])
        ready = sem("ready")
        seen = sem("seen")
        consts = sem("consts")
        total = sem("total")
        plan = sem("plan")
        filled = sem("filled")
        x_in = [sem(f"x_in{k}") for k in range(2)]
        x_full, xt_done = sem("x_full"), sem("xt_done")
        taken = sem("taken")
        g_full, u_full = sem("g_full"), sem("u_full")
        g_done, h_done = sem("g_done"), sem("h_done")
        h_full, ht_done = sem("h_full"), sem("ht_done")
        y_full, y_done = sem("y_full"), sem("y_done")
        sent = [sem(f"sent{k}") for k in range(2)]
        loads = [(wd[:], d["wd"].rearrange("(c p) n -> p c n", p=P)), (ident[:], d["ident"]),
                 (ones_sq[:], d["ones_sq"]), (list_at[:], d["list_at"]), (tile_no[:], d["tile_no"]),
                 (padding[:], d["padding"])]
        PLANNED = 12
        block = ctx.enter_context(nc.Block())

        @block.sync
        def _(sp):
            for a, b in loads[1:] + loads[:1]:
                sp.dma_start(a, b).then_inc(consts, 16)
            sp.wait_ge(consts, 16 * len(loads))
            for n in range(E1):
                at = E1 * CAP + n * P
                sp.dma_start(lists[at:at + P, :], padding[:, E1 + n]).then_inc(filled, 16)
            sp.wait_ge(plan, PLANNED)
            for e in range(E1):
                at = sp.value_load(fill_i[0:1, e:e + 1], min_val=0, max_val=E1 * CAP)
                sp.dma_start(lists[bass.ds(at, P), :], padding[:, e]).then_inc(filled, 16)
            sp.wait_ge(filled, 16 * 2 * E1)

            def load(k, span):
                at = sp.value_load(row_i[0:1, span], min_val=0, max_val=E1 * CAP + E1 * P - P)
                sp.dma_start(x[:, k], lists[bass.ds(at, P), :]).then_inc(x_in[k], 16)

            load(0, slice(0, 1))
            load(1, slice(1, 2))
            with sp.Fori(1, ROWS1 // 2) as i:
                for k in range(2):
                    sp.wait_ge(x_full, 2 * i + k - 1)
                    sp.wait_ge(taken, 2 * i + k - 1)
                    load(k, bass.ds(2 * i + k, 1))

        @block.gpsimd
        def _(pool):
            nc.gpsimd.memset(gspot[:], 0.0).then_inc(ready, 1)
            pool.wait_ge(ready, 1)
            with pool.Fori(0, ROWS1 // 2) as i:
                for k in range(2):
                    pool.wait_ge(y_done, 2 * i + k + 1)
                    carry_pool(pool, gspot[:, k]).then_inc(seen, 1)
                    pool.indirect_dma_start(
                        out=results, out_offset=bass.IndirectOffsetOnAxis(ap=dest[:, k:k + 1], axis=0),
                        in_=y[:, k, :], in_offset=None).then_inc(sent[k], 16)
            for k in range(2):
                pool.wait_ge(sent[k], 16 * (ROWS1 // 2))

        def scalar_tile(act, T, k, first=False, last=False):
            act.wait_ge(g_full, T + 1)
            if not first:
                act.wait_ge(h_done, T - 1)
            nc.scalar.activation(gate[:, k], gp[k][:], ACT.Silu).then_inc(g_done, 1)
            if not last:
                act.wait_ge(x_full, T + 2)
                nc.scalar.activation(xt[:, 1 - k], xp[:, 0:DM].rearrange("p (c n) -> p c n", c=KC), ACT.Copy)\
                    .then_inc(xt_done, 1)
            act.wait_ge(h_full, T + 1)
            nc.scalar.activation(ht[:, k], hp[:].rearrange("p (c n) -> p c n", c=HC), ACT.Copy).then_inc(ht_done, 1)

        @block.scalar
        def _(act):
            act.wait_ge(x_full, 1)
            nc.scalar.activation(xt[:, 0], xp[:, 0:DM].rearrange("p (c n) -> p c n", c=KC), ACT.Copy)\
                .then_inc(xt_done, 1)
            scalar_tile(act, 0, 0, first=True)
            with act.Fori(0, LOOP) as i:
                for k in (1, 0):
                    scalar_tile(act, 2 * i + 2 - k, k)
            scalar_tile(act, ROWS1 - 1, 1, last=True)

        def vector_hidden(dve, T, k):
            dve.wait_ge(u_full, T + 1)
            dve.wait_ge(g_done, T + 1)
            nc.vector.tensor_tensor(h[:, k], gate[:, k], up[k][:], ALU.mult).then_inc(h_done, 1)

        def vector_last_columns(dve, k, n):
            dve.wait_ge(x_in[k], 16 * n + 16)
            dve.wait_ge(sent[k], 16 * n)
            nc.vector.tensor_copy(weight[:, k:k + 1], x[:, k, DM + 1:DM + 2])
            nc.vector.tensor_copy(dest[:, k:k + 1], x[:, k, DM:DM + 1]).then_inc(taken, 1)

        def vector_out(dve, T, k, n):
            dve.wait_ge(seen, 2 * n)
            dve.wait_ge(taken, T + 1)
            dve.wait_ge(y_full, T + 1)
            nc.vector.tensor_scalar(y[:, k], yp[:, 0:DM], weight[:, k:k + 1], None, ALU.mult)\
                .then_inc(y_done, 1)

        @block.vector
        def _(dve):
            step = [0]

            def work(ins):
                step[0] += 1
                ins.then_inc(plan, 1)
                dve.wait_ge(plan, step[0])

            dve.wait_ge(consts, 16 * len(loads))
            dve.wait_ge(total, 1)
            work(nc.vector.tensor_scalar(count_i[:], tp[:, 0:E1], float(P - 1), None, ALU.add))
            work(nc.vector.tensor_scalar(tiles_i[:], count_i[:], 7, None, ALU.logical_shift_right))
            work(nc.vector.tensor_copy(tiles_of[:], tiles_i[:]))
            work(nc.vector.memset(ones_row[:], 1.0))
            work(nc.vector.tensor_tensor_scan(ends[:], ones_row[:], tiles_of[:], 0.0, ALU.mult, ALU.add))
            nc.vector.tensor_tensor(fill_i[:], tp[:, 0:E1], list_at[:], ALU.add)
            work(nc.vector.tensor_tensor(passed[:, 0], tile_no[:].unsqueeze(2).broadcast_to([P, ROWS1, E1]),
                                         ends[:].unsqueeze(1).broadcast_to([P, ROWS1, E1]), ALU.is_ge))
            work(nc.vector.tensor_tensor(passed[:, 1], passed[:, 0],
                                         tiles_of[:].unsqueeze(1).broadcast_to([P, ROWS1, E1]), ALU.mult))
            work(nc.vector.tensor_reduce(of_tile[:, 0:2], passed[:], AX.X, ALU.add))
            work(nc.vector.tensor_tensor(of_tile[:, 2], tile_no[:], of_tile[:, 1], ALU.subtract))
            nc.vector.tensor_scalar(of_tile[:, 3], of_tile[:, 0], float(CAP), None, ALU.mult)
            work(nc.vector.tensor_scalar(of_tile[:, 4], of_tile[:, 2], float(P), None, ALU.mult))
            work(nc.vector.tensor_scalar(expert_i[:], of_tile[:, 0], float(E1 - 1), None, ALU.min))
            work(nc.vector.tensor_tensor(row_i[:], of_tile[:, 3], of_tile[:, 4], ALU.add))
            assert step[0] == PLANNED, step
            vector_hidden(dve, 0, 0)
            vector_last_columns(dve, 0, 0)
            with dve.Fori(0, LOOP) as i:
                for k in (1, 0):
                    T = 2 * i + 2 - k
                    vector_hidden(dve, T, k)
                    vector_last_columns(dve, k, i + 1 - k)
                    vector_out(dve, T - 1, 1 - k, i)
            vector_hidden(dve, ROWS1 - 1, 1)
            vector_last_columns(dve, 1, LOOP)
            vector_out(dve, ROWS1 - 2, 0, LOOP)
            vector_out(dve, ROWS1 - 1, 1, LOOP)

        @block.tensor
        def _(pe):
            mm, tr = nc.tensor.matmul, nc.tensor.transpose
            pe.wait_ge(consts, 16 * len(loads))
            mm(tp[:, 0:E1], ones_sq[:], listed, start=True, stop=True).then_inc(total, 1)
            pe.wait_ge(plan, PLANNED)
            pe.wait_ge(w_in, 64)
            wd_flat = wd[:].rearrange("p a n -> p (a n)")

            def rows_in(k, n):
                pe.wait_ge(x_in[k], 16 * n + 16)
                for c in range(KC):
                    ins = tr(xp[:, c * P:(c + 1) * P], x[:, k, c * P:(c + 1) * P], ident[:])
                ins.then_inc(x_full, 1)

            def inward(T, k, at, first=False):
                e = pe.value_load(expert_i[0:1, at], min_val=0, max_val=E1 - 1)
                pe.wait_ge(xt_done, T + 1)
                if not first:
                    pe.wait_ge(h_done, T - 1)
                for out, w, full in ((gp, wg, g_full), (up, wu, u_full)):
                    for c in range(KC):
                        ins = mm(out[k][:], xt[:, k, c], w[:, c, bass.ds(e * H1, H1)], start=c == 0, stop=c == KC - 1)
                    ins.then_inc(full, 1)

            def turn(T, k, first=False):
                pe.wait_ge(h_done, T + 1)
                if not first:
                    pe.wait_ge(ht_done, T)
                for c in range(HC):
                    ins = tr(hp[:, c * P:(c + 1) * P], h[:, k, c * P:(c + 1) * P], ident[:])
                ins.then_inc(h_full, 1)

            def outward(T, k, at):
                e = pe.value_load(expert_i[0:1, at], min_val=0, max_val=E1 - 1)
                pe.wait_ge(ht_done, T + 1)
                pe.wait_ge(y_done, T)
                for c in range(HC):
                    ins = mm(yp[:, 0:DM], ht[:, k, c], wd_flat[:, bass.ds(e * (HC * DM) + c * DM, DM)],
                             start=c == 0, stop=c == HC - 1)
                ins.then_inc(y_full, 1)

            rows_in(0, 0)
            inward(0, 0, slice(0, 1), first=True)
            rows_in(1, 0)
            turn(0, 0, first=True)
            with pe.Fori(0, LOOP) as i:
                for k in (1, 0):
                    T = 2 * i + 2 - k
                    inward(T, k, bass.ds(T, 1))
                    outward(T - 1, 1 - k, bass.ds(T - 1, 1))
                    rows_in(1 - k, i + 1)
                    turn(T, k)
            T = ROWS1 - 1
            inward(T, 1, slice(T, T + 1))
            outward(T - 1, 0, slice(T - 1, T))
            turn(T, 1)
            outward(T, 1, slice(T, T + 1))


def final_phase(nc, sems, src, results, out_rows):
    with ExitStack() as ctx:
        def sb(name, shape):
            return ctx.enter_context(nc.sbuf_tensor(f"f_{name}", shape, F32))

        def sem(name):
            return take(nc, sems, f"f_{name}")

        R = 4
        x = sb("x", [P, R, SUB, DM])
        y = sb("y", [P, R, K1, SUB, DM])
        stats = sb("stats", [P, SUB, 6])
        mv = sb("mv", [P, SUB, 4])
        half = sb("half", [P, 1])
        eps = sb("eps", [P, 1])
        loaded = [sem(f"loaded{k}") for k in range(R)]
        ready = sem("ready")
        chain = sem("chain")
        mv_done, ve_done, rstd = sem("mv_done"), sem("ve_done"), sem("rstd")
        out_done, sent = sem("out_done"), [sem(f"sent{k}") for k in range(R)]
        block = ctx.enter_context(nc.Block())

        def tiled(rows):
            return rows.rearrange("(t p) n -> p t n", p=P)

        @block.sync
        def _(sp):
            for T in range(TILES):
                k = T % R
                if T >= R:
                    sp.wait_ge(sent[k], 16 * (T // R))
                sp.dma_start(x[:, k], tiled(src[T * TOK:(T + 1) * TOK, :])).then_inc(loaded[k], 16)
                for c in range(K1):
                    at = c * NT + T * TOK
                    sp.dma_start(y[:, k, c], tiled(results[at:at + TOK, :])).then_inc(loaded[k], 16)

        @block.scalar
        def _(act):
            for T in range(TILES):
                act.wait_ge(out_done, T + 1)
                act.dma_start(tiled(out_rows[T * TOK:(T + 1) * TOK, :]), x[:, T % R]).then_inc(sent[T % R], 16)
            for k in range(R):
                act.wait_ge(sent[k], 16 * (TILES // R))

        @block.gpsimd
        def _(pool):
            nc.gpsimd.memset(half[:], -0.5)
            nc.gpsimd.memset(eps[:], LN_EPS).then_inc(ready, 1)
            pool.wait_ge(ready, 1)
            for T in range(TILES):
                pool.wait_ge(mv_done, T + 1)
                nc.gpsimd.tensor_tensor(mv[:, :, 2], mv[:, :, 1], eps[:].broadcast_to([P, SUB]), ALU.add)\
                    .then_inc(ve_done, 1)
                pool.wait_ge(ve_done, T + 1)
                nc.gpsimd.tensor_tensor(mv[:, :, 3], mv[:, :, 2], half[:].broadcast_to([P, SUB]), ALU.pow)\
                    .then_inc(rstd, 1)

        @block.vector
        def _(dve):
            n = 0
            for T in range(TILES):
                k = T % R
                dve.wait_ge(loaded[k], 48 * (T // R + 1))
                for c in range(K1):
                    nc.vector.tensor_tensor(x[:, k], x[:, k], y[:, k, c], ALU.add).then_inc(chain, 1)
                    n += 1
                    dve.wait_ge(chain, n)
                for t in range(SUB):
                    ins = nc.vector.bn_stats(stats[:, t], x[:, k, t])
                ins.then_inc(chain, 1)
                n += 1
                dve.wait_ge(chain, n)
                for t in range(SUB):
                    ins = nc.vector.bn_aggr(mv[:, t, 0:2], stats[:, t])
                ins.then_inc(mv_done, 1)
                dve.wait_ge(rstd, T + 1)
                for t in range(SUB):
                    ins = nc.vector.tensor_scalar(x[:, k, t], x[:, k, t], mv[:, t, 0:1], mv[:, t, 3:4],
                                                  ALU.subtract, ALU.mult)
                ins.then_inc(out_done, 1)


def decoder(nc, a, out):
    def scratch(name, shape):
        return nc.dram_tensor(name, shape, F32, kind="Internal").ap()

    res1, res1_t, cw1 = scratch("res1", [NT, DM]), scratch("res1_t", [DM, NT]), scratch("cw1", [E0, NT])
    mid = scratch("mid", [NT, DM])
    res2 = scratch("res2", [NT, DM])
    lists = scratch("lists", [E1 * CAP + E1 * P, ROW])
    results = scratch("results", [K1 * NT + 2 * E1 * P, DM])
    layer0 = {k: a[k] for k in ("ident", "head_mask", "ctx_t", "ctx", "decay", "decay_q", "decay_k", "decay_s",
                                "block_mask")}
    layer0.update(wq=a["L0_wq"], wk=a["L0_wk"], wv=a["L0_wv"], wo=a["L0_wo"], wout=a["L0_wout"], bout=a["L0_bout"],
                  router=a["L0_router"], router_b=a["L0_router_b"], b2=a["L0_b2"], sb2=a["L0_sb2"])
    layer1 = {k: a[k] for k in ("ident", "head_mask", "ctx_t", "causal", "iota", "before", "ones_sq",
                                "list_at", "dest")}
    layer1.update(wq1=a["L1_mq"], wk1=a["L1_mk"], wv1=a["L1_mv"], wo1=a["L1_mo"], gate=a["L1_gate"],
                  memory=a["L1_memory"], mem_norm=a["L1_norm"], mem_norm_rows=a["L1_norm_rows"],
                  wq=a["L1_wq"], wk=a["L1_wk"], wv=a["L1_wv"], wout=a["L1_wout"], bout=a["L1_bout"],
                  router=a["L1_router"])
    with ExitStack() as ctx:
        big = ctx.enter_context(nc.sbuf_tensor("big", [P, 4 * 4096 + 5120], F32))
        sems = []

        def end_phase():
            nc.clear_and_free_semaphores(sems)
            nc.all_engine_barrier()
            sems.clear()

        w_in = ctx.enter_context(nc.semaphore("w_in"))
        listed = ctx.enter_context(nc.sbuf_tensor("listed", [P, E1], F32))
        halves = [big[:, n * 8192:(n + 1) * 8192] for n in range(2)]
        spare = big[:, 16384:]
        as_cols = [t.rearrange("p (c n) -> p c n", c=KC) for t in halves]
        w2 = halves[1].rearrange("p (c n) -> p c n", n=DM)

        def load_layer0(sp):
            sp.dma_start(as_cols[0], a["L0_w1"].rearrange("(c p) n -> p c n", p=P)).then_inc(w_in, 16)
            sp.dma_start(w2, a["L0_w2"].rearrange("(c p) n -> p c n", p=P)).then_inc(w_in, 16)

        def load_layer1(sp):
            for t, name in zip(as_cols, ("L1_wg", "L1_wu")):
                sp.dma_start(t, a[name].rearrange("(c p) n -> p c n", p=P)).then_inc(w_in, 16)

        attention_phase(nc, sems, 0, layer0, a["x"], a["x_t"], res1, res1_t, cw1, E0, 8, load_layer0, spare)
        end_phase()
        shared_routed_phase(nc, sems, dict(sw1=a["L0_sw1"], sw2=a["L0_sw2"], b1=a["L0_b1"], sb1=a["L0_sb1"]),
                            as_cols[0], w2, w_in, res1, res1_t, cw1, mid)
        end_phase()
        attention_phase(nc, sems, 1, layer1, mid.rearrange("(b s) n -> b s n", b=NB), None, res2, None, None, E1, K1,
                        load_layer1, spare, lists, listed[:])
        end_phase()
        gated_phase(nc, sems, dict(wd=a["L1_wd"], **{k: a[k] for k in ("ident", "ones_sq", "list_at", "tile_no",
                                                                       "padding")}),
                    as_cols[0], as_cols[1], w_in, lists, listed[:], results)
        end_phase()
        final_phase(nc, sems, res2, results, out)


def shape_constants():
    gamma = 1.0 - 2.0 ** (-5.0 - np.arange(RH))
    at = np.arange(P)
    diff = at[None, :] - at[:, None]
    table = np.where(diff >= 0, gamma[:, None, None] ** np.maximum(diff, 0), 0.0) * RD ** -0.5
    return {
        "ident": np.eye(P),
        "head_mask": at[:, None] // XD == np.arange(P // XD)[None, :],
        "decay": table.reshape(2, 4, P, P).transpose(2, 1, 0, 3),
        "decay_q": (np.repeat(gamma, RD)[:, None] ** (at[None, :] + 1) * RD ** -0.5).reshape(2, P, P)
        .transpose(1, 0, 2),
        "decay_k": np.repeat(gamma, RD)[None, :] ** (P - 1 - at[:, None]),
        "decay_s": (np.repeat(gamma, RD) ** P).reshape(2, P).T,
        "block_mask": at[:, None] // RD == at[None, :] // RD,
        "causal": diff >= 0,
        "iota": np.broadcast_to(np.arange(E1), (P, E1)),
        "before": diff > 0,
        "ones_sq": np.ones((P, P)),
        "list_at": np.broadcast_to(np.arange(E1) * CAP, (P, E1)),
        "tile_no": np.broadcast_to(np.arange(ROWS1), (P, ROWS1)),
        "dest": at[:, None, None] + np.arange(NB)[None, :, None] * SEQ + np.arange(K1)[None, None, :] * NT,
        "padding": np.where(np.arange(ROW) == DM, K1 * NT + np.arange(2 * E1)[None, :, None] * P + at[:, None, None],
                            0),
    }


def kernel(**inputs):
    import concourse.bacc as _bacc
    from concourse.bass_utils import run_bass_kernel_spmd as _run

    t = {k: np.asarray(v) for k, v in inputs.items()}
    laid = {
        "x": t["x"], "x_t": t["x"].transpose(0, 2, 1), "ctx": t["ctx_1024"], "ctx_t": t["ctx_1024"].transpose(0, 2, 1),
        "L0_wq": t["L0_attn_Wq"], "L0_wk": t["L0_attn_Wk"], "L0_wv": t["L0_attn_Wv"], "L0_wo": t["L0_attn_Wo"],
        "L0_wout": t["L0_xattn_W_out"].T, "L0_bout": np.broadcast_to(t["L0_xattn_b_out"], (P, DM)),
        "L0_router": t["L0_ffn_router_w"], "L0_router_b": t["L0_ffn_router_b"].reshape(1, E0),
        "L0_w1": t["L0_ffn_w1"].transpose(1, 0, 2).reshape(DM, E0 * H0),
        "L0_b1": t["L0_ffn_b1"].reshape(E0 // 2, P).T,
        "L0_w2": t["L0_ffn_w2"].reshape(E0 * H0, DM), "L0_b2": t["L0_ffn_b2"],
        "L0_sw1": t["L0_ffn_sw1"], "L0_sb1": t["L0_ffn_sb1"].reshape(ES * HS // P, P).T,
        "L0_sw2": t["L0_ffn_sw2"], "L0_sb2": np.broadcast_to(t["L0_ffn_sb2"], (P, ES, DM)),
        "L1_mq": t["L1_attn_w_q"].T, "L1_mk": t["L1_attn_w_k"].T, "L1_mv": t["L1_attn_w_v"].T,
        "L1_mo": t["L1_attn_w_o"].T, "L1_gate": np.broadcast_to(t["L1_attn_gate"], (P, 1)),
        "L1_memory": t["L1_attn_memory"], "L1_norm": t["L1_attn_memory_norm"].reshape(MEM, 1),
        "L1_norm_rows": np.broadcast_to(t["L1_attn_memory_norm"], (P, MEM)),
        "L1_wq": t["L1_xattn_W_q"], "L1_wk": t["L1_xattn_W_k"], "L1_wv": t["L1_xattn_W_v"],
        "L1_wout": t["L1_xattn_W_o"], "L1_bout": np.broadcast_to(t["L1_xattn_b_o"], (P, DM)),
        "L1_router": t["L1_ffn_router_w"].T,
        "L1_wg": t["L1_ffn_w_gate"].transpose(2, 0, 1).reshape(DM, E1 * H1),
        "L1_wu": t["L1_ffn_w_up"].transpose(2, 0, 1).reshape(DM, E1 * H1),
        "L1_wd": t["L1_ffn_w_down"].transpose(0, 2, 1).reshape(E1 * H1, DM),
    }
    laid.update({k: v.astype(np.float32) for k, v in shape_constants().items()})
    nc = _bacc.Bacc("TRN2", target_bir_lowering=False, num_devices=1)
    arrays, aps = {}, {}
    for name, array in laid.items():
        arrays[f"in_{name}"] = np.ascontiguousarray(array)
        aps[name] = nc.dram_tensor(f"in_{name}", array.shape, F32, kind="ExternalInput").ap()
    out = nc.dram_tensor("out", (NT, DM), F32, kind="ExternalOutput").ap()
    decoder(nc, aps, out)
    r = _run(nc, [arrays], core_ids=[0])
    return r.results[0]["out"].reshape(NB, SEQ, DM)
```
